# Optimizing a Trainium2 kernel written in Bass

```python
import numpy as np
import jax
import jax.numpy as jnp

def _softmax(x, axis=-1):
    return jax.nn.softmax(x, axis=axis)

def _gelu(x):
    return jax.nn.gelu(x, approximate=True)

def _silu(x):
    return jax.nn.silu(x)

def _sigmoid(x):
    return jax.nn.sigmoid(x)

def _layernorm(x, axis=-1, eps=1e-05):
    m = jnp.mean(x, axis=axis, keepdims=True)
    v = jnp.var(x, axis=axis, keepdims=True)
    return (x - m) / jnp.sqrt(v + eps)

def _scatter_add(tgt, idx, src, axis=0):
    return tgt.at[idx].add(src)

def _segment_sum(src, seg, n):
    return jax.ops.segment_sum(src, seg, n)
kernel_name = 'mk_adj_preln_d2_adj_r2_45198a'

def setup_inputs(seed: int=0):
    np.random.seed(seed)
    _w = jnp.asarray

    def _rec_inputs():
        import jax
        import jax.numpy as jnp
        _gk = jax.random.key(seed)
        x = -0.000929 + 1 * jax.random.normal(jax.random.fold_in(_gk, 1), (4096, 128), jnp.float32)
        _a = jax.random.bernoulli(jax.random.fold_in(_gk, 2), 0.000488281, (4096, 4096))
        _a = jnp.logical_or(_a, jnp.swapaxes(_a, -1, -2))
        _a = jnp.logical_or(_a, jnp.eye(4096, dtype=bool))
        adj = _a.astype(jnp.int32)
        return (x, adj)
    x, adj = _rec_inputs()

    def _L0_gnn_setup():
        import jax, jax.numpy as jnp
        import numpy as np
        from jax import lax
        N = 4096
        D = 128
        CHUNK = 128
        key = jax.random.key(seed)
        k1, k2 = jax.random.split(key)
        x = jax.random.normal(k1, (N, D), dtype=jnp.float32)
        adj = jax.random.randint(k2, (N, N), 0, 2, dtype=jnp.int32)
        return {'x': x, 'adj': adj}
    _L0_gnn_all = _L0_gnn_setup()
    _L0_gnn_in = {k: v for k, v in _L0_gnn_all.items() if k in ()}
    del _L0_gnn_all

    def _L1_gnn_setup():
        import jax, jax.numpy as jnp
        import numpy as np
        N = 6144
        IN_DIM = 128
        OUT_DIM = 128
        LR_SLOPE = 0.01
        NEG_INF = -9e+16
        key = jax.random.key(seed)
        k1, k2, k3, k4 = jax.random.split(key, 4)
        emb_mat = jax.random.normal(k1, (N, IN_DIM), dtype=jnp.float32)
        adj_mat = jax.random.randint(k2, (N, N), 0, 2, dtype=jnp.int32)
        W = jax.random.normal(k3, (OUT_DIM, IN_DIM), dtype=jnp.float32) * (2.0 / (IN_DIM + OUT_DIM)) ** 0.5
        a = jax.random.normal(k4, (2 * OUT_DIM, 1), dtype=jnp.float32) * (2.0 / (2 * OUT_DIM + 1)) ** 0.5
        return {'emb_mat': emb_mat, 'adj_mat': adj_mat, 'W': W, 'a': a}
    _L1_gnn_all = _L1_gnn_setup()
    _L1_gnn_in = {k: v for k, v in _L1_gnn_all.items() if k in ('W', 'a')}
    del _L1_gnn_all
    return {'x': x, 'adj': adj, 'L1_gnn_W': _L1_gnn_in['W'], 'L1_gnn_a': _L1_gnn_in['a']}

def reference(x, adj, L1_gnn_W, L1_gnn_a):
    import jax
    import jax.numpy as jnp

    def _L0_gnn_ref(x, adj):
        import jax, jax.numpy as jnp
        import numpy as np
        from jax import lax
        N = 4096
        D = 128
        CHUNK = 128
        n, d = x.shape
        neg = jnp.finfo(x.dtype).min
        adj_chunks = adj.reshape(n // CHUNK, CHUNK, n)

        def step(carry, a):
            mask = a != 0
            masked = jnp.where(mask[:, :, None], x[None, :, :], neg)
            m = jnp.max(masked, axis=1)
            has_nbr = jnp.any(mask, axis=1)
            out = jnp.where(has_nbr[:, None], m, jnp.zeros((), x.dtype))
            return (carry, out)
        _, out = lax.scan(step, None, adj_chunks)
        return out.reshape(n, d)

    def _L1_gnn_ref(emb_mat, adj_mat, W, a):
        import jax, jax.numpy as jnp
        import numpy as np
        N = 6144
        IN_DIM = 128
        OUT_DIM = 128
        LR_SLOPE = 0.01
        NEG_INF = -9e+16
        out_dim = W.shape[0]
        e_new = emb_mat @ W.T
        a1 = a[:out_dim, :]
        a2 = a[out_dim:, :]
        source_scores = e_new @ a1
        target_scores = e_new @ a2
        e = source_scores + target_scores.T
        e = jax.nn.leaky_relu(e, negative_slope=LR_SLOPE)
        e = jnp.where(adj_mat > 0, e, NEG_INF)
        attention = jax.nn.softmax(e, axis=-1)
        e_transf = attention @ e_new
        return jax.nn.relu(e_transf)
    h = jnp.maximum(_layernorm(x, axis=-1), 0.0)
    x = x + _L0_gnn_ref(h, adj)
    h = jnp.maximum(_layernorm(x, axis=-1), 0.0)
    x = x + _L1_gnn_ref(h, adj, L1_gnn_W, L1_gnn_a)
    return x

_drawn_inputs = setup_inputs


def setup_inputs(seed=0):
    import zlib

    import numpy as np

    out = dict(_drawn_inputs(seed))
    spreads = {}
    factors = {}
    for name, (base, spread) in spreads.items():
        noise = np.random.default_rng([zlib.crc32(name.encode()), seed]).standard_normal(out[name].shape)
        drawn = base * np.exp(spread * noise) if base else spread * noise
        out[name] = jnp.asarray(drawn.astype(out[name].dtype))
    for name, factor in factors.items():
        out[name] = (out[name] * factor).astype(out[name].dtype)
    return out
```

```python
import concourse.bass as bass
from concourse import mybir
from contextlib import ExitStack

F32, I32 = mybir.dt.float32, mybir.dt.int32
BF16, F16 = mybir.dt.bfloat16, mybir.dt.float16
ALU = mybir.AluOpType
ACT = mybir.ActivationFunctionType
AX = mybir.AxisListType.X

P = 128
N = 4096
T = N // P
D = 128
HALF = N // 2
GROUPS = 256
BITS = N // GROUPS
LEVELS = 3
SLOTS = 16
BLOCKS = 5
EDGES = BLOCKS * P
ROWLEN = D + 2
EW = D + 1
NEG_SLOPE = 0.01
EPS = 1e-5
HMAX = 64.0
BIG = 1e30
MASKED = -9e16
SKEW = 3

C_ID, C_TRI, C_ROW1, C_IOTA, C_G = 0, P, 2 * P, 3 * P, 3 * P + EDGES
C_PB = C_G + GROUPS
C_S = C_PB + BLOCKS
C_P1 = C_S + SLOTS
CONSTS = C_P1 + 1


def constants():
    import numpy as np
    c = np.zeros((P, CONSTS), np.float32)
    p = np.arange(P, dtype=np.float32)[:, None]
    c[:, C_ID:C_ID + P] = np.eye(P)
    c[:, C_TRI:C_TRI + P] = np.triu(np.ones((P, P)), 1)
    c[:, C_ROW1:C_ROW1 + P] = np.arange(P)[None] + 1
    c[:, C_IOTA:C_IOTA + EDGES] = np.arange(EDGES)[None]
    c[:, C_G:C_G + GROUPS] = np.arange(GROUPS)[None]
    c[:, C_PB:C_PB + BLOCKS] = p + P * np.arange(BLOCKS)[None]
    c[:, C_S:C_S + SLOTS] = np.arange(SLOTS)[None]
    c[:, C_P1:C_P1 + 1] = p + 1
    return c


class Chain:

    def __init__(self, eng, sem):
        self.eng, self.sem, self.n, self.seen = eng, sem, 0, 0
        eng.sem_inc(sem)
        eng.sem_clear(sem)

    def did(self, ins, wait=True):
        ins.then_inc(self.sem, 1)
        self.n += 1
        if wait:
            self.wait()

    def wait(self):
        if self.seen < self.n:
            self.eng.wait_ge(self.sem, self.n)
        self.seen = self.n


def build(nc, x, adj, W, a, consts, out, h_rows, e_rows):
    ctx = ExitStack()
    with ctx:
        def sb(name, shape, dt=F32):
            return ctx.enter_context(nc.sbuf_tensor(name, shape, dt))

        def ps(name, cols):
            return ctx.enter_context(nc.psum_tensor(name, [P, cols], F32))

        def sem(name):
            return ctx.enter_context(nc.semaphore(name))

        cst = sb("cst", [P, CONSTS])
        ident = cst[:, C_ID:C_ID + P]
        row1 = cst[:, C_ROW1:C_ROW1 + P]
        edge_pb = cst[:, C_PB:C_PB + BLOCKS]
        slot_iota = cst[:, C_S:C_S + SLOTS]
        code_w = sb("code_w", [P, BITS + 1, P], BF16)
        iota_g = sb("iota_g", [P, GROUPS], BF16)
        not_eye = sb("not_eye", [P, P], BF16)
        tri = sb("tri", [P, P], F16)
        iota_e = sb("iota_e", [P, EDGES], F16)
        cut_w = sb("cut_w", [P, P], F16)
        adj_in = sb("adj_in", [P, 2, N], I32)
        mask = sb("mask", [P, 2, N], BF16)
        X = sb("X", [P, T, D])
        H = sb("H", [P, T, D])
        EN = sb("EN", [P, T, D + 2])
        G = sb("G", [P, 4, BLOCKS, EW])
        stat6 = sb("stat6", [P, 6])
        mv = sb("mv", [P, T, 2])
        mv1 = sb("mv1", [P, 2])
        std = sb("std", [P, T])
        rstd = sb("rstd", [P, T])
        eps = sb("eps", [P, 1])
        nmr = sb("nmr", [P, T])
        deg = sb("deg", [P, T, 2])
        cnt = sb("cnt", [P, T])
        start = sb("start", [P, T])
        end = sb("end", [P, T])
        least = sb("least", [P, T])
        rest = sb("rest", [P, T])
        last_row = sb("last_row", [P, T, BLOCKS])
        idx_all = sb("idx_all", [P, T, BLOCKS], I32)
        idx = [sb(f"idx{q}", [P, BLOCKS], I32) for q in range(4)]
        top = sb("top", [P, SLOTS])
        keys2 = sb("keys2", [P, GROUPS])
        topi = sb("topi", [P, SLOTS], I32)
        grp = sb("grp", [P, SLOTS], I32)
        powr = sb("powr", [P, LEVELS, SLOTS], I32)
        rem = sb("rem", [P, LEVELS, SLOTS])
        shf = sb("shf", [P, LEVELS, SLOTS], I32)
        cand = sb("cand", [P, LEVELS * SLOTS])
        cand2 = sb("cand2", [P, LEVELS * SLOTS])
        val = sb("val", [P, SLOTS])
        valid = sb("valid", [P, SLOTS])
        V = sb("V", [P, 20], F16)
        ge_s = sb("ge_s", [P, EDGES], F16)
        ge_e = sb("ge_e", [P, EDGES], F16)
        R = sb("R", [P, EDGES], F16)
        eq_s = sb("eq_s", [P, EDGES], F16)
        kpos = sb("kpos", [P, BLOCKS])
        onehot = sb("onehot", [P, BLOCKS, SLOTS])
        pick = sb("pick", [P, BLOCKS, SLOTS])
        red = sb("red", [P, BLOCKS])
        lastm = sb("lastm", [P, BLOCKS])
        cut = sb("cut", [P, 2, EDGES], BF16)
        scan = sb("scan", [P, EDGES])
        scanT = sb("scanT", [P, BLOCKS, P])
        S = sb("S", [P, BLOCKS, P])
        agg = sb("agg", [P, D])
        h1 = sb("h1", [P, D])
        h1T = sb("h1T", [P, P])
        WX = sb("WX", [P, D + 2])
        Wsb = sb("Wsb", [P, D])
        asb = sb("asb", [P, 2])
        z = sb("z", [P, EDGES])
        off_s, off_e, off = (sb(n, [P, EDGES], BF16) for n in ("off_s", "off_e", "off"))
        prob = sb("prob", [P, 2, EDGES])
        probT = sb("probT", [P, 2, BLOCKS, P])
        zmax = sb("zmax", [P, 1])
        neg_max = sb("neg_max", [P, 2])
        xself = sb("xself", [P, T])
        wself = sb("wself", [P, 2])
        den = sb("den", [P, 2])
        dn = sb("dn", [P, 2])
        num = sb("num", [P, 2, D])
        O = sb("O", [P, 2, D])
        junk = sb("junk", [P, 2 * T])

        bad = sb("bad", [P, 5, T])
        bad_row = sb("bad_row", [P, 1])
        general = sb("general", [P, 1], I32)
        ones = sb("ones", [P, P])
        row_in = adj_in
        hT = EN[:, :, :].rearrange("p t d -> p (t d)")[:, 0:N]
        wide = mask[:, :, :].rearrange("p q n -> p (q n)").bitcast(F32)
        e_wide = adj_in[:, 1, :].bitcast(F32)
        t_all = H[:, :, :].rearrange("p t d -> p (t d)")
        aggT = h1T

        key_ps = ps("key_ps", 512)
        emb_ps = ps("emb_ps", 512)
        list_ps = ps("list_ps", 512)
        gt_ps = ps("gt_ps", 1024)
        back_ps = ps("back_ps", 1024)
        seg_ps = ps("seg_ps", 512)
        LB = list_ps[:, 8:8 + 20 * BLOCKS].rearrange("p (b v) -> p b v", v=20)

        cst_in, x_in, w_in = sem("cst_in"), [sem(f"x_in{c}") for c in range(4)], sem("w_in")
        cst_made = sem("cst_made")
        adj_loaded = [[sem(f"adj_loaded{q}{h}") for h in range(2)] for q in range(2)]
        signed = sem("signed")
        diag_cleared = sem("diag_cleared")
        keys_made, keys_taken = sem("keys_made"), sem("keys_taken")
        counted, start_made, spans_made = sem("counted"), sem("start_made"), sem("spans_made")
        lists_made, lists_taken = sem("lists_made"), sem("lists_taken")
        idx_ready = sem("idx_ready")
        cut_made, cut_saved = sem("cut_made"), sem("cut_saved")
        gathered = [[sem(f"gathered{q}_{b}") for b in range(BLOCKS)] for q in range(4)]
        gt_made, scanned = sem("gt_made"), sem("scanned")
        back_made, back_saved = sem("back_made"), sem("back_saved")
        ends_made, seg_made, seg_taken = sem("ends_made"), sem("seg_made"), sem("seg_taken")
        x1_stats, std1_made, rstd1_made, h1_made, h1T_made, h1T_saved = (sem("x1_stats"), sem("std1_made"), sem("rstd1_made"), sem("h1_made"), sem("h1T_made"), sem("h1T_saved"))
        emb_made, emb_saved, emb_stored = sem("emb_made"), sem("emb_saved"), [sem("emb_stored0"), sem("emb_stored1")]
        std0_made = sem("std0_made")
        stats0, h0_made, h0_stored = sem("stats0"), sem("h0_made"), sem("h0_stored")
        wx_ps_made, wx_saved = sem("wx_ps_made"), sem("wx_saved")
        c_ln, c_set, c_keys, c_span, c_list, c_seg = (sem(n) for n in ("c_ln", "c_set", "c_keys", "c_span", "c_list", "c_seg"))
        idx2_ready, tb_made, z_made, m_made = sem("idx2_ready"), sem("tb_made"), sem("z_made"), sem("m_made")
        c_z, c_fin = sem("c_z"), sem("c_fin")
        prob_made, probT_made, probT_saved, num_made, num_taken = (sem(n) for n in ("prob_made", "probT_made", "probT_saved", "num_made", "num_taken"))
        self_made, selfw_made = sem("self_made"), sem("selfw_made")
        out_made, out_stored = sem("out_made"), [sem("out_stored0"), sem("out_stored1")]

        passed = {"pool": sem("pool_passed"), "dve": sem("dve_passed")}

        def settled(eng, who):
            eng.sem_inc(passed[who])

        checked, bad_summed, flag_made = sem("checked"), sem("bad_summed"), sem("flag_made")
        gx_in, gh_ready, ghT_ps = sem("gx_in"), sem("gh_ready"), sem("ghT_ps")
        grow_in = [sem("grow_in0"), sem("grow_in1")]
        grow_used, gmax_made, gagg_made, gagg_taken = sem("grow_used"), sem("gmax_made"), sem("gagg_made"), sem("gagg_taken")
        c_gen = sem("c_gen")
        gvar_made, gstd_made, gh1_made, gh1T_ps, gh1T_saved = (sem(n) for n in ("gvar_made", "gstd_made", "gh1_made", "gh1T_ps", "gh1T_saved"))
        gemb_ps, gt_ps_made = sem("gemb_ps"), sem("gt_ps_made")
        gadj_in, gadj_used, gmax1_made, gprob_made = (sem(n) for n in ("gadj_in", "gadj_used", "gmax1_made", "gprob_made"))
        gt_ready, gprob_ready = sem("gt_ready"), sem("gprob_ready")
        gprobT_ps, gprobT_saved, gnum_made, gout_made, gout_stored = (sem(n) for n in ("gprobT_ps", "gprobT_saved", "gnum_made", "gout_made", "gout_stored"))

        block = ctx.enter_context(nc.Block())

        x_v = x.rearrange("(t p) d -> p t d", p=P)
        out_v = out.rearrange("(t p) d -> p t d", p=P)
        h_v = h_rows.rearrange("(t p) d -> p t d", p=P)
        e_v = e_rows.rearrange("(t p) d -> p t d", p=P)
        adj_v = adj.rearrange("(t p) n -> p t n", p=P)

        def wait(eng, s, value):
            if isinstance(value, int) and value <= 0:
                return
            eng.wait_ge(s, value)

        def looped(eng, step, lo, hi, unroll):
            with eng.Fori(0, (hi - lo) // unroll) as turn:
                for u in range(unroll):
                    step(turn * unroll + (lo + u), (lo + u) % unroll)

        def steps(eng, step, last, lead, ahead, unroll=2):
            lo = lead
            hi = T - ahead
            hi -= (hi - lo) % unroll
            for i in range(lo):
                step(i, i % unroll)
            looped(eng, step, lo, hi, unroll)
            for i in range(hi, last):
                step(i, i % unroll)

        def within(i, off):
            return not isinstance(i, int) or 0 <= i + off < T

        XC = 4
        TC = T // XC

        def flag(eng):
            eng.wait_ge(flag_made, 1)
            return eng.value_load(general[0:1, 0:1], min_val=0, max_val=1 << 20)

        def tile(buf, t, cols=slice(None)):
            return buf[:, bass.ds(t, 1), cols].rearrange("p a d -> p (a d)")

        @block.sync
        def _(sp):
            sp.dma_start(cst[:, :], consts).then_inc(cst_in, 16)
            for c in range(XC):
                sp.dma_start(X[:, c * TC:(c + 1) * TC, :], x_v[:, c * TC:(c + 1) * TC, :]).then_inc(x_in[c], 16)
            sp.dma_start(Wsb[:, :], W).then_inc(w_in, 16)
            for h in range(2):
                sp.dma_start(asb[:, h:h + 1], a[h * P:(h + 1) * P, :]).then_inc(w_in, 16)

            def load(t, q):
                for h in range(2):
                    wait(sp, signed, (t - 2) * 2 + h + 1)
                    sp.dma_start(adj_in[:, q, h * HALF:(h + 1) * HALF],
                                 adj_v[:, bass.ds(t, 1), h * HALF:(h + 1) * HALF].rearrange("p a n -> p (a n)")).then_inc(adj_loaded[q][h], 16)

            load(0, 0)
            load(1, 1)
            for c in range(XC):
                sp.wait_ge(h0_made, (c + 1) * TC)
                sp.dma_start(h_v[:, c * TC:(c + 1) * TC, :], H[:, c * TC:(c + 1) * TC, :]).then_inc(h0_stored, 16)

            def step(i, q):
                if within(i, 2):
                    load(i + 2, q)
                if within(i, -SKEW - 1):
                    t = i - SKEW - 1
                    sp.wait_ge(emb_saved, t + 1)
                    sp.dma_start(e_v[:, bass.ds(t, 1), 0:D + 2].rearrange("p a d -> p (a d)"),
                                 EN[:, bass.ds(t, 1), :].rearrange("p a d -> p (a d)")).then_inc(emb_stored[(q + SKEW + 1) % 2], 16)
            steps(sp, step, T + SKEW + 1, 4, 2)

            def store(i, q):
                sp.wait_ge(out_made, i + 1)
                sp.dma_start(out_v[:, bass.ds(i, 1), :].rearrange("p a d -> p (a d)"), O[:, q, :]).then_inc(out_stored[q], 16)
            looped(sp, store, 0, T, 2)
            for q in range(2):
                sp.wait_ge(out_stored[q], 16 * T // 2)

            with sp.If(flag(sp) > 0):
                sp.dma_start(X[:, :, :], x_v).then_inc(gx_in, 16)
                with sp.Fori(0, N // 2) as pair:
                    sp.wait_ge(grow_used, pair * 2 + 1)
                    for u in range(2):
                        sp.dma_start(row_in[:, u, :], adj[bass.ds(pair * 2 + u, 1), :].broadcast_to([P, N])).then_inc(grow_in[u], 16)
                with sp.Fori(0, T) as t:
                    sp.wait_ge(gadj_used, t + 1)
                    sp.dma_start(row_in[:, 0, :], tile(adj_v, t)).then_inc(gadj_in, 16)
                    sp.wait_ge(gout_made, t + 1)
                    sp.dma_start(tile(out_v, t), O[:, 0, :]).then_inc(gout_stored, 16)
                sp.wait_ge(gout_stored, 16 * T + 16)

        @block.gpsimd
        def _(pool):
            pool.wait_ge(h0_stored, 16 * XC)

            def step(i, q):
                pool.wait_ge(idx_ready, i + 1)
                wait(pool, gt_made, i - 1)
                settled(pool, "pool")
                for b in range(BLOCKS):
                    pool.indirect_dma_start(out=G[:, q, b, 0:D], out_offset=None, in_=h_rows,
                                            in_offset=bass.IndirectOffsetOnAxis(ap=idx[q][:, b:b + 1], axis=0)).then_inc(gathered[q][b], 16)
            for i in range(2):
                step(i, i)
            looped(pool, step, 2, T, 2)
            for q in range(2):
                pool.wait_ge(emb_stored[q], 16 * T // 2)

            def step1(i, q):
                pool.wait_ge(idx2_ready, i + 1)
                wait(pool, num_made, i - 3)
                settled(pool, "pool")
                for b in range(BLOCKS):
                    pool.indirect_dma_start(out=G[:, q, b, :], out_offset=None, in_=e_rows,
                                            in_offset=bass.IndirectOffsetOnAxis(ap=idx[q][:, b:b + 1], axis=0)).then_inc(gathered[q][b], 16)
            for i in range(4):
                step1(i, i)
            looped(pool, step1, 4, T, 4)

        @block.scalar
        def _(act):
            def sign(t, q, h):
                act.wait_ge(adj_loaded[q][h], (t - q) * 8 + 16)
                wait(act, keys_made, t - 1)
                act.activation(mask[:, q, h * HALF:(h + 1) * HALF], adj_in[:, q, h * HALF:(h + 1) * HALF], ACT.Sign,
                               accum_out=deg[:, bass.ds(t, 1), h:h + 1].rearrange("p a b -> p (a b)")).then_inc(signed, 1)

            sign(0, 0, 0)
            sign(0, 0, 1)
            for c in range(XC):
                ts = slice(c * TC, (c + 1) * TC)
                act.wait_ge(c_ln, 2 * TC * (c + 1))
                act.activation(std[:, ts], mv[:, ts, 1], ACT.Sqrt, bias=eps[:, :]).then_inc(std0_made, 1)
            for c in range(XC):
                act.wait_ge(stats0, c + 1)
                for t in range(c * TC, (c + 1) * TC):
                    act.activation(H[:, t, :], X[:, t, :], ACT.Relu, bias=nmr[:, t:t + 1], scale=rstd[:, t:t + 1]).then_inc(h0_made, 1)
            sign(1, 1, 0)
            sign(1, 1, 1)
            act.wait_ge(wx_ps_made, 1)
            act.activation(WX[:, :], emb_ps[:, 0:D + 2], ACT.Copy).then_inc(wx_saved, 1)

            def step(i, q):
                if within(i, 2):
                    sign(i + 2, q, 0)
                if within(i, -2):
                    t = i - 2
                    act.wait_ge(back_made, t + 1)
                    wait(act, seg_made, t)
                    act.activation(scanT[:, :, :].rearrange("p b d -> p (b d)"), back_ps[:, 0:EDGES], ACT.Copy).then_inc(back_saved, 1)
                if within(i, 2):
                    sign(i + 2, q, 1)
                if within(i, 0):
                    act.wait_ge(cut_made, i + 1)
                    wait(act, scanned, i - 1)
                    act.activation(cut[:, q, :], back_ps[:, 0:EDGES], ACT.Copy).then_inc(cut_saved, 1)
                if within(i, -3):
                    t = i - 3
                    act.wait_ge(x1_stats, t + 1)
                    act.activation(std[:, bass.ds(t, 1)], mv1[:, 1:2], ACT.Sqrt, bias=eps[:, :]).then_inc(std1_made, 1)
                    wait(act, h1T_made, t)
                    act.activation(h1[:, :], X[:, bass.ds(t, 1), :].rearrange("p a d -> p (a d)"), ACT.Relu,
                                   bias=nmr[:, bass.ds(t, 1)]).then_inc(h1_made, 1)
                    act.wait_ge(h1T_made, t + 1)
                    wait(act, emb_made, t)
                    act.activation(h1T[:, :], emb_ps[:, 0:P], ACT.Copy).then_inc(h1T_saved, 1)
                    act.wait_ge(emb_made, t + 1)
                    act.wait_ge(rstd1_made, t + 1)
                    act.activation(EN[:, bass.ds(t, 1), :].rearrange("p a d -> p (a d)"), emb_ps[:, P:P + D + 2], ACT.Copy, scale=rstd[:, bass.ds(t, 1)]).then_inc(emb_saved, 1)
            steps(act, step, T + SKEW, 4, 2)

            def step1(i, q):
                if within(i, -1):
                    t = i - 1
                    act.wait_ge(probT_made, t + 1)
                    wait(act, num_made, t - 1)
                    act.activation(probT[:, 1 - q, :, :].rearrange("p b d -> p (b d)"), gt_ps[:, 0:EDGES], ACT.Copy).then_inc(probT_saved, 1)
                if within(i, 0):
                    act.wait_ge(m_made, i + 1)
                    wait(act, num_taken, i - 1)
                    act.activation(prob[:, q, :], prob[:, q, :], ACT.Exp, bias=neg_max[:, q:q + 1], accum_out=den[:, q:q + 1])
                    act.activation(wself[:, q:q + 1], xself[:, bass.ds(i, 1)], ACT.Exp, bias=neg_max[:, q:q + 1]).then_inc(prob_made, 1)
            act.wait_ge(self_made, 1)
            for i in range(2):
                step1(i, i)
            looped(act, step1, 2, T, 2)
            step1(T, 0)

            with act.If(flag(act) > 0):
                with act.Fori(0, T) as t:
                    act.wait_ge(gvar_made, t + 1)
                    act.activation(std[:, bass.ds(t, 1)], mv1[:, 1:2], ACT.Sqrt, bias=eps[:, :]).then_inc(gstd_made, 1)
                    act.activation(h1[:, :], tile(X, t), ACT.Relu, bias=nmr[:, bass.ds(t, 1)]).then_inc(gh1_made, 1)
                    act.wait_ge(gh1T_ps, t + 1)
                    act.activation(h1T[:, :], emb_ps[:, 0:P], ACT.Copy).then_inc(gh1T_saved, 1)
                with act.Fori(0, T) as t:
                    act.wait_ge(gmax1_made, t + 1)
                    act.activation(e_wide, e_wide, ACT.Exp, bias=neg_max[:, 0:1], accum_out=den[:, 0:1]).then_inc(gprob_made, 1)

        @block.vector
        def _(dve):
            dve.wait_ge(cst_in, 16)
            for k in range(BITS):
                dve.tensor_scalar(code_w[:, k, :], ident, float(2 ** (k + 8)), None, ALU.mult)
            dve.tensor_copy(code_w[:, BITS, :], ident)
            dve.tensor_copy(iota_g[:, :], cst[:, C_G:C_G + GROUPS])
            dve.tensor_scalar(not_eye[:, :], ident, -1.0, 1.0, ALU.mult, ALU.add)
            dve.tensor_copy(tri[:, :], cst[:, C_TRI:C_TRI + P])
            dve.tensor_copy(iota_e[:, :], cst[:, C_IOTA:C_IOTA + EDGES])
            dve.tensor_copy(V[:, 17:18], cst[:, C_P1:C_P1 + 1])
            dve.memset(eps[:, :], EPS)
            dve.memset(cut_w[:, :], -HMAX).then_inc(cst_made, 1)
            dve.wait_ge(cst_made, 1)

            def row_stats(link, t, mean_var):
                link.did(dve.bn_stats(stat6[:, :], X[:, bass.ds(t, 1), :].rearrange("p a d -> p (a d)")))
                link.did(dve.bn_aggr(mean_var, stat6[:, :]))

            link = Chain(dve, c_ln)
            for c in range(XC):
                dve.wait_ge(x_in[c], 16)
                for t in range(c * TC, (c + 1) * TC):
                    row_stats(link, t, mv[:, t, :])
            for c in range(XC):
                ts = slice(c * TC, (c + 1) * TC)
                dve.wait_ge(std0_made, c + 1)
                link.did(dve.reciprocal(rstd[:, ts], std[:, ts]))
                dve.scalar_tensor_tensor(nmr[:, ts], mv[:, ts, 0], -1.0, rstd[:, ts], ALU.mult, ALU.mult).then_inc(stats0, 1)
            link.wait()

            def clear_diagonal(t, q):
                dve.wait_ge(signed, 2 * t + 2)
                blk = mask[:, q, bass.ds(t * P, P)]
                dve.tensor_tensor(blk, blk, not_eye[:, :], ALU.mult).then_inc(diag_cleared, 1)

            def read_keys(t):
                dve.wait_ge(keys_made, t + 1)
                keys = key_ps[:, 0:GROUPS]
                link = Chain(dve, c_keys)
                link.did(dve.max(top[:, 0:8], keys))
                link.did(dve.match_replace(keys2[:, :], top[:, 0:8], keys, -1.0))
                dve.tensor_reduce(least[:, bass.ds(t, 1)], keys, AX, ALU.min).then_inc(keys_taken, 1)
                link.did(dve.max(top[:, 8:16], keys2[:, :]))
                link.did(dve.tensor_copy(topi[:, :], top[:, :]), wait=False)
                prev = top
                rest_ = top[:, :]
                for v in range(LEVELS):
                    link.did(dve.tensor_scalar(powr[:, v, :], rest_.bitcast(I32), 0x7F800000, None, ALU.bitwise_and))
                    link.did(dve.tensor_tensor(rem[:, v, :], rest_, powr[:, v, :].bitcast(F32), ALU.subtract))
                    rest_ = rem[:, v, :]
                link.did(dve.tensor_reduce(rest[:, bass.ds(t, 1)], rem[:, LEVELS - 1, :], AX, ALU.max), wait=False)
                link.did(dve.tensor_scalar(grp[:, :], topi[:, :], GROUPS - 1, None, ALU.bitwise_and), wait=False)
                link.did(dve.tensor_scalar(shf[:, :, :], powr[:, :, :], 15, None, ALU.logical_shift_right))
                link.did(dve.scalar_tensor_tensor(cand[:, :].rearrange("p (v s) -> p v s", v=LEVELS), shf[:, :, :],
                                                  float(1 - (127 + 8) * GROUPS),
                                                  grp[:, :].rearrange("p (v s) -> p v s", v=1).broadcast_to([P, LEVELS, SLOTS]),
                                                  ALU.add, ALU.add))
                link.did(dve.max(val[:, 0:8], cand[:, :]))
                link.did(dve.match_replace(cand2[:, :], val[:, 0:8], cand[:, :], -1.0))
                link.did(dve.max(val[:, 8:16], cand2[:, :]))
                link.did(dve.tensor_scalar(valid[:, :], val[:, :], 0.0, None, ALU.is_gt))
                link.did(dve.tensor_reduce(cnt[:, bass.ds(t, 1)], valid[:, :], AX, ALU.add))
                link.did(dve.tensor_scalar(V[:, 0:SLOTS], val[:, :], 1.0, -float(N // 2 + 1), ALU.max, ALU.add), wait=False)
                dve.tensor_copy(V[:, 18:19], cnt[:, bass.ds(t, 1)]).then_inc(counted, 1)
                link.wait()

            def spans(t):
                dve.wait_ge(start_made, t + 1)
                wait(dve, cut_made, t)
                link = Chain(dve, c_span)
                link.did(dve.tensor_copy(start[:, bass.ds(t, 1)], list_ps[:, 0:1]))
                link.did(dve.tensor_copy(V[:, 16:17], start[:, bass.ds(t, 1)]), wait=False)
                link.did(dve.tensor_tensor(end[:, bass.ds(t, 1)], start[:, bass.ds(t, 1)], cnt[:, bass.ds(t, 1)], ALU.add))
                link.did(dve.tensor_scalar(ge_s[:, :], iota_e[:, :], start[:, bass.ds(t, 1)], None, ALU.is_ge), wait=False)
                link.did(dve.tensor_scalar(eq_s[:, :], iota_e[:, :], start[:, bass.ds(t, 1)], None, ALU.is_equal), wait=False)
                link.did(dve.tensor_scalar(ge_e[:, :], iota_e[:, :], end[:, bass.ds(t, 1)], None, ALU.is_ge))
                dve.tensor_tensor(R[:, :], ge_s[:, :], ge_e[:, :], ALU.subtract).then_inc(spans_made, 1)
                link.wait()

            def edge_list(t, q):
                dve.wait_ge(lists_made, t + 1)
                link = Chain(dve, c_list)
                def over_slots(v):
                    return v.rearrange("p (b s) -> p b s", s=1).broadcast_to([P, BLOCKS, SLOTS])
                link.did(dve.tensor_tensor(kpos[:, :], edge_pb, LB[:, :, 16], ALU.subtract))
                link.did(dve.tensor_tensor(onehot[:, :, :], slot_iota.rearrange("p (b s) -> p b s", b=1).broadcast_to([P, BLOCKS, SLOTS]),
                                           over_slots(kpos[:, :]), ALU.is_equal))
                link.did(dve.tensor_tensor(pick[:, :, :], onehot[:, :, :], LB[:, :, 0:SLOTS], ALU.mult))
                link.did(dve.scalar_tensor_tensor(lastm[:, :], kpos[:, :], 1.0, LB[:, :, 18], ALU.add, ALU.is_equal))
                link.did(dve.tensor_reduce(red[:, :], pick[:, :, :], AX, ALU.add), wait=False)
                dve.tensor_tensor(last_row[:, bass.ds(t, 1), :].rearrange("p a b -> p (a b)"), lastm[:, :], LB[:, :, 17], ALU.mult).then_inc(lists_taken, 1)
                link.wait()
                dve.tensor_scalar(idx[q][:, :], red[:, :], float(N // 2), None, ALU.add).then_inc(idx_ready, 1)
                link.did(dve.tensor_scalar(idx_all[:, bass.ds(t, 1), :].rearrange("p a b -> p (a b)"), red[:, :], float(N // 2), None, ALU.add), wait=False)
                link.wait()

            def segment_max(t, q):
                dve.wait_ge(gt_made, t + 1)
                dve.wait_ge(cut_saved, t + 1)
                wait(dve, back_made, t)
                dve.tensor_tensor_scan(scan[:, :], cut[:, q, :], gt_ps[:, 0:EDGES], 0.0, ALU.add, ALU.max).then_inc(scanned, 1)

            def row_ends(t):
                wait(dve, seg_made, t)
                for b in range(BLOCKS):
                    ins = dve.tensor_scalar(S[:, b, :], row1, last_row[:, bass.ds(t, 1), b:b + 1].rearrange("p a b -> p (a b)"), None, ALU.is_equal)
                ins.then_inc(ends_made, 1)

            def residual(t):
                dve.wait_ge(seg_made, t + 1)
                link = Chain(dve, c_seg)
                tt = bass.ds(t, 1)
                xt = X[:, tt, :].rearrange("p a d -> p (a d)")
                dve.tensor_tensor(agg[:, :], seg_ps[:, 0:D], H[:, tt, :].rearrange("p a d -> p (a d)"), ALU.max).then_inc(seg_taken, 1)
                dve.wait_ge(seg_taken, t + 1)
                link.did(dve.tensor_tensor(xt, xt, agg[:, :], ALU.add))
                wait(dve, std1_made, t)
                settled(dve, "dve")
                row_stats(link, t, mv1[:, :])
                dve.tensor_scalar(nmr[:, tt], mv1[:, 0:1], -1.0, None, ALU.mult).then_inc(x1_stats, 1)
                link.wait()

            def inverse_std(t):
                dve.wait_ge(std1_made, t + 1)
                dve.reciprocal(rstd[:, bass.ds(t, 1)], std[:, bass.ds(t, 1)]).then_inc(rstd1_made, 1)

            dve.memset(ones[:, :], 1.0)
            clear_diagonal(0, 0)

            def step(i, q):
                if within(i, 0):
                    read_keys(i)
                if within(i, 1):
                    clear_diagonal(i + 1, 1 - q)
                if within(i, -2):
                    segment_max(i - 2, q)
                if within(i, 0):
                    spans(i)
                if within(i, -2):
                    row_ends(i - 2)
                if within(i, -3):
                    residual(i - 3)
                if within(i, 0):
                    edge_list(i, q)
                if within(i, -3):
                    inverse_std(i - 3)
            steps(dve, step, T + SKEW, 4, 1)

            link = Chain(dve, c_set)
            link.did(dve.tensor_tensor(bad[:, 0, :], deg[:, :, 0], deg[:, :, 1], ALU.add))
            link.did(dve.tensor_tensor(bad[:, 0, :], bad[:, 0, :], cnt[:, :], ALU.subtract))
            link.did(dve.tensor_scalar(bad[:, 0, :], bad[:, 0, :], 1.0, None, ALU.not_equal), wait=False)
            link.did(dve.tensor_scalar(bad[:, 1, :], cnt[:, :], float(SLOTS), None, ALU.is_ge), wait=False)
            link.did(dve.tensor_scalar(bad[:, 2, :], least[:, :], 0.0, None, ALU.is_lt), wait=False)
            link.did(dve.tensor_scalar(bad[:, 3, :], rest[:, :], float(GROUPS), None, ALU.is_ge), wait=False)
            link.did(dve.tensor_scalar(bad[:, 4, :], end[:, :], float(EDGES), None, ALU.is_gt))
            dve.tensor_reduce(bad_row[:, :], bad[:, :, :].rearrange("p c t -> p (c t)"), AX, ALU.add).then_inc(checked, 1)
            dve.wait_ge(bad_summed, 1)
            dve.tensor_copy(general[:, :], list_ps[:, 0:1]).then_inc(flag_made, 1)

            dve.wait_ge(emb_saved, T)
            tgt, src = EN[:, :, D], EN[:, :, D + 1]
            link = Chain(dve, c_set)
            link.did(dve.tensor_tensor(junk[:, 0:T], tgt, src, ALU.add))
            dve.scalar_tensor_tensor(xself[:, :], junk[:, 0:T], NEG_SLOPE, junk[:, 0:T], ALU.mult, ALU.max).then_inc(self_made, 1)

            def copy_idx(t, q):
                wait(dve, tb_made, t - 3)
                dve.tensor_copy(idx[q][:, :], idx_all[:, bass.ds(t, 1), :].rearrange("p a b -> p (a b)")).then_inc(idx2_ready, 1)

            def scores(t, q):
                tt = bass.ds(t, 1)
                link = Chain(dve, c_z)
                link.did(dve.tensor_scalar(off_s[:, :], iota_e[:, :], start[:, tt], -BIG, ALU.is_lt, ALU.mult), wait=False)
                link.did(dve.tensor_scalar(off_e[:, :], iota_e[:, :], end[:, tt], -BIG, ALU.is_ge, ALU.mult))
                link.did(dve.tensor_tensor(off[:, :], off_s[:, :], off_e[:, :], ALU.add))
                dve.wait_ge(tb_made, t + 1)
                dve.scalar_tensor_tensor(z[:, :], back_ps[:, 0:EDGES], EN[:, tt, D + 1:D + 2].rearrange("p a d -> p (a d)"),
                                         off[:, :], ALU.add, ALU.add).then_inc(z_made, 1)
                wait(dve, probT_made, t - 1)
                dve.wait_ge(z_made, t + 1)
                link.did(dve.scalar_tensor_tensor(prob[:, q, :], z[:, :], NEG_SLOPE, z[:, :], ALU.mult, ALU.max))
                wait(dve, prob_made, t - 1)
                link.did(dve.tensor_reduce(zmax[:, :], prob[:, q, :], AX, ALU.max))
                dve.tensor_scalar(neg_max[:, q:q + 1], zmax[:, :], xself[:, tt], -1.0, ALU.max, ALU.mult).then_inc(m_made, 1)

            def finish(t, q):
                tt = bass.ds(t, 1)
                dve.wait_ge(num_made, t + 1)
                dve.wait_ge(prob_made, t + 1)
                link = Chain(dve, c_fin)
                link.did(dve.tensor_tensor(dn[:, 0:1], den[:, q:q + 1], wself[:, q:q + 1], ALU.add))
                link.did(dve.reciprocal(dn[:, 1:2], dn[:, 0:1]), wait=False)
                dve.scalar_tensor_tensor(num[:, 0, :], EN[:, tt, 0:D].rearrange("p a d -> p (a d)"), wself[:, q:q + 1],
                                         seg_ps[:, 0:D], ALU.mult, ALU.add).then_inc(num_taken, 1)
                dve.wait_ge(num_taken, t + 1)
                link.wait()
                link.did(dve.tensor_scalar(num[:, 1, :], num[:, 0, :], dn[:, 1:2], 0.0, ALU.mult, ALU.max))
                if not isinstance(t, int) or t >= 2:
                    dve.wait_ge(out_stored[q], (t - q) * 8)
                dve.tensor_tensor(O[:, q, :], num[:, 1, :], X[:, tt, :].rearrange("p a d -> p (a d)"), ALU.add).then_inc(out_made, 1)
                link.wait()

            for t in range(4):
                copy_idx(t, t)

            def step1(i, q):
                if within(i, 0):
                    scores(i, q % 2)
                if within(i, 4) and not (isinstance(i, int) and i + 4 >= T):
                    copy_idx(i + 4, q)
                if within(i, -1):
                    finish(i - 1, (q + 1) % 2)
            for i in range(4):
                step1(i, i)
            looped(dve, step1, 4, T - 4, 4)
            for i in range(T - 4, T + 1):
                step1(i, i % 4)

            with dve.If(flag(dve) > 0):
                dve.sem_inc(grow_used)
                dve.sem_inc(gout_stored, 16)
                with dve.Fori(0, T) as t:
                    link = Chain(dve, c_gen)
                    link.did(dve.tensor_copy(h1[:, :], tile(H, t)))
                    dve.sem_inc(gh_ready)
                    dve.wait_ge(ghT_ps, t + 1)
                    link.did(dve.tensor_copy(hT[:, bass.ds(t * P, P)], emb_ps[:, 0:P]))
                dve.wait_ge(gx_in, 16)
                with dve.Fori(0, T) as t:
                    with dve.Fori(0, P // 2) as pair:
                        for u in range(2):
                            dve.wait_ge(grow_in[u], (t * (P // 2) + pair) * 16 + 16)
                            link = Chain(dve, c_gen)
                            link.did(dve.scalar_tensor_tensor(wide, row_in[:, u, :], 0.0, hT, ALU.not_equal, ALU.mult))
                            dve.sem_inc(grow_used)
                            link.did(dve.tensor_reduce(aggT[:, bass.ds(pair * 2 + u, 1)], wide, AX, ALU.max))
                    dve.sem_inc(gmax_made)
                    dve.wait_ge(gagg_made, t + 1)
                    link = Chain(dve, c_gen)
                    link.did(dve.tensor_tensor(tile(X, t), tile(X, t), seg_ps[:, 0:D], ALU.add))
                    dve.sem_inc(gagg_taken)
                with dve.Fori(0, T) as t:
                    link = Chain(dve, c_gen)
                    row_stats(link, t, mv1[:, :])
                    link.did(dve.tensor_scalar(nmr[:, bass.ds(t, 1)], mv1[:, 0:1], -1.0, None, ALU.mult))
                    dve.sem_inc(gvar_made)
                    dve.wait_ge(gstd_made, t + 1)
                    link.did(dve.reciprocal(rstd[:, bass.ds(t, 1)], std[:, bass.ds(t, 1)]))
                    dve.wait_ge(gemb_ps, t + 1)
                    link.did(dve.tensor_scalar(tile(EN, t), emb_ps[:, P:P + D + 2], rstd[:, bass.ds(t, 1)], None, ALU.mult))
                    link.did(dve.tensor_copy(zmax[:, :], tile(EN, t, slice(D, D + 1))))
                    dve.sem_inc(gt_ready)
                    dve.wait_ge(gt_ps_made, t + 1)
                    link.did(dve.tensor_copy(t_all[:, bass.ds(t * P, P)], seg_ps[:, 0:P]))
                dve.sem_inc(gadj_used)
                with dve.Fori(0, T) as t:
                    dve.wait_ge(gadj_in, t * 16 + 16)
                    link = Chain(dve, c_gen)
                    link.did(dve.tensor_scalar(e_wide, t_all, tile(EN, t, slice(D + 1, D + 2)), None, ALU.add))
                    link.did(dve.scalar_tensor_tensor(e_wide, e_wide, NEG_SLOPE, e_wide, ALU.mult, ALU.max))
                    link.did(dve.scalar_tensor_tensor(e_wide, row_in[:, 0, :], 0.0, e_wide, ALU.is_gt, ALU.mult))
                    link.did(dve.tensor_scalar(wide, row_in[:, 0, :], 0.0, 1.0, ALU.is_gt, ALU.subtract))
                    link.did(dve.scalar_tensor_tensor(e_wide, wide, -MASKED, e_wide, ALU.mult, ALU.add))
                    dve.sem_inc(gadj_used)
                    link.did(dve.tensor_reduce(zmax[:, :], e_wide, AX, ALU.max))
                    link.did(dve.tensor_scalar(neg_max[:, 0:1], zmax[:, :], -1.0, None, ALU.mult))
                    dve.sem_inc(gmax1_made)
                    dve.wait_ge(gprob_made, t + 1)
                    settled(dve, "dve")
                    with dve.Fori(0, T) as j:
                        link = Chain(dve, c_gen)
                        link.did(dve.tensor_copy(h1[:, :], e_wide[:, bass.ds(j * P, P)]))
                        dve.sem_inc(gprob_ready)
                        dve.wait_ge(gprobT_ps, t * T + j + 1)
                        link.did(dve.tensor_copy(h1T[:, :], emb_ps[:, 0:P]))
                        dve.sem_inc(gprobT_saved)
                    dve.wait_ge(gnum_made, t + 1)
                    link = Chain(dve, c_gen)
                    link.did(dve.reciprocal(dn[:, 1:2], den[:, 0:1]))
                    link.did(dve.tensor_scalar(num[:, 1, :], seg_ps[:, 0:D], dn[:, 1:2], 0.0, ALU.mult, ALU.max))
                    dve.wait_ge(gout_stored, t * 16 + 16)
                    link.did(dve.tensor_tensor(O[:, 0, :], num[:, 1, :], tile(X, t), ALU.add))
                    dve.sem_inc(gout_made)

        @block.tensor
        def _(pe):
            pe.wait_ge(cst_made, 1)
            pe.wait_ge(w_in, 48)
            pe.transpose(emb_ps[:, 0:D], Wsb[:, :], ident)
            pe.matmul(emb_ps[:, D:D + 1], Wsb[:, :], asb[:, 1:2], start=True, stop=True)
            pe.matmul(emb_ps[:, D + 1:D + 2], Wsb[:, :], asb[:, 0:1], start=True, stop=True).then_inc(wx_ps_made, 1)

            def codes(t, q):
                pe.wait_ge(diag_cleared, t + 1)
                wait(pe, keys_taken, t)
                for k in range(BITS):
                    pe.matmul(key_ps[:, 0:GROUPS], code_w[:, k, :], mask[:, q, k * GROUPS:(k + 1) * GROUPS], start=(k == 0), stop=False)
                pe.matmul(key_ps[:, 0:GROUPS], code_w[:, BITS, :], iota_g[:, :], start=False, stop=True).then_inc(keys_made, 1)
            codes(0, 0)

            def step(i, q):
                if within(i, -2):
                    t = i - 2
                    wait(pe, scanned, t)
                    for b in range(BLOCKS):
                        pe.wait_ge(gathered[q][b], (t - q) * 8 + 16)
                        ins = pe.transpose(gt_ps[:, b * P:(b + 1) * P], G[:, q, b, 0:D], ident)
                    ins.then_inc(gt_made, 1)
                if within(i, 0):
                    pe.wait_ge(counted, i + 1)
                    wait(pe, lists_taken, i)
                    pe.matmul(list_ps[:, 0:1], tri[:, :], V[:, 18:19], start=True, stop=True).then_inc(start_made, 1)
                if within(i, 1):
                    codes(i + 1, 1 - q)
                if within(i, -2):
                    t = i - 2
                    pe.wait_ge(scanned, t + 1)
                    wait(pe, cut_saved, t + 2 if not isinstance(i, int) else min(t + 2, T))
                    for b in range(BLOCKS):
                        ins = pe.transpose(back_ps[:, b * P:(b + 1) * P], scan[:, b * P:(b + 1) * P], ident)
                    ins.then_inc(back_made, 1)
                if within(i, 0):
                    pe.wait_ge(spans_made, i + 1)
                    for b in range(BLOCKS):
                        ins = pe.matmul(list_ps[:, 8 + 20 * b:8 + 20 * b + 19], R[:, b * P:(b + 1) * P], V[:, 0:19], start=True, stop=True)
                    ins.then_inc(lists_made, 1)
                    if within(i, -2):
                        pe.wait_ge(back_saved, i - 1)
                    else:
                        wait(pe, cut_saved, i)
                    pe.matmul(back_ps[:, 0:512], cut_w[:, :], eq_s[:, 0:512], start=True, stop=True)
                    pe.matmul(back_ps[:, 512:EDGES], cut_w[:, :], eq_s[:, 512:EDGES], start=True, stop=True).then_inc(cut_made, 1)
                if within(i, -2):
                    t = i - 2
                    pe.wait_ge(back_saved, t + 1)
                    pe.wait_ge(ends_made, t + 1)
                    wait(pe, seg_taken, t)
                    for b in range(BLOCKS):
                        ins = pe.matmul(seg_ps[:, 0:D], S[:, b, :], scanT[:, b, :], start=(b == 0), stop=(b == BLOCKS - 1))
                    ins.then_inc(seg_made, 1)
                if within(i, -3):
                    t = i - 3
                    pe.wait_ge(h1_made, t + 1)
                    if isinstance(t, int) and t == 0:
                        pe.wait_ge(wx_saved, 1)
                    wait(pe, emb_saved, t)
                    pe.transpose(emb_ps[:, 0:P], h1[:, :], ident).then_inc(h1T_made, 1)
                    pe.wait_ge(h1T_saved, t + 1)
                    pe.matmul(emb_ps[:, P:P + D + 2], h1T[:, :], WX[:, :], start=True, stop=True).then_inc(emb_made, 1)
            steps(pe, step, T + SKEW, 4, 1)

            pe.wait_ge(checked, 1)
            pe.matmul(list_ps[:, 0:1], ones[:, :], bad_row[:, :], start=True, stop=True).then_inc(bad_summed, 1)

            def step1(i, q):
                if within(i, 0):
                    wait(pe, z_made, i)
                    for b in range(BLOCKS):
                        pe.wait_ge(gathered[q][b], (i - q) * 4 + 16 * (T // 2 if q < 2 else 0) + 16)
                        ins = pe.matmul(back_ps[:, b * P:(b + 1) * P], G[:, q, b, D:D + 1].broadcast_to([P, P]), ident, start=True, stop=True)
                    ins.then_inc(tb_made, 1)
                if within(i, -1):
                    t = i - 1
                    pe.wait_ge(prob_made, t + 1)
                    wait(pe, probT_saved, t)
                    for b in range(BLOCKS):
                        ins = pe.transpose(gt_ps[:, b * P:(b + 1) * P], prob[:, (q + 1) % 2, b * P:(b + 1) * P], ident)
                    ins.then_inc(probT_made, 1)
                    pe.wait_ge(probT_saved, t + 1)
                    wait(pe, num_taken, t)
                    for b in range(BLOCKS):
                        ins = pe.matmul(seg_ps[:, 0:D], probT[:, (q + 1) % 2, b, :], G[:, (q + 3) % 4, b, 0:D], start=(b == 0), stop=(b == BLOCKS - 1))
                    ins.then_inc(num_made, 1)
            for i in range(4):
                step1(i, i)
            looped(pe, step1, 4, T, 4)
            step1(T, 0)

            with pe.If(flag(pe) > 0):
                with pe.Fori(0, T) as t:
                    pe.wait_ge(gh_ready, t + 1)
                    pe.transpose(emb_ps[:, 0:P], h1[:, :], ident).then_inc(ghT_ps, 1)
                with pe.Fori(0, T) as t:
                    pe.wait_ge(gmax_made, t + 1)
                    pe.transpose(seg_ps[:, 0:D], aggT[:, :], ident).then_inc(gagg_made, 1)
                with pe.Fori(0, T) as t:
                    pe.wait_ge(gh1_made, t + 1)
                    pe.transpose(emb_ps[:, 0:P], h1[:, :], ident).then_inc(gh1T_ps, 1)
                    pe.wait_ge(gh1T_saved, t + 1)
                    pe.matmul(emb_ps[:, P:P + D + 2], h1T[:, :], WX[:, :], start=True, stop=True).then_inc(gemb_ps, 1)
                    pe.wait_ge(gt_ready, t + 1)
                    pe.matmul(seg_ps[:, 0:P], zmax[:, 0:1].broadcast_to([P, P]), ident, start=True, stop=True).then_inc(gt_ps_made, 1)
                with pe.Fori(0, T) as t:
                    def product(j, first, last):
                        pe.wait_ge(gprob_ready, t * T + j + 1)
                        pe.transpose(emb_ps[:, 0:P], h1[:, :], ident).then_inc(gprobT_ps, 1)
                        pe.wait_ge(gprobT_saved, t * T + j + 1)
                        ins = pe.matmul(seg_ps[:, 0:D], h1T[:, :], tile(EN, j, slice(0, D)), start=first, stop=last)
                        if last:
                            ins.then_inc(gnum_made, 1)
                    product(0, True, False)
                    with pe.Fori(0, T - 2) as j:
                        product(j + 1, False, False)
                    product(T - 1, False, True)


def kernel(**inputs):
    import numpy as _np
    import concourse.bacc as _bacc
    from concourse import mybir as _mybir
    from concourse.bass_utils import run_bass_kernel_spmd as _run

    nc = _bacc.Bacc("TRN2", target_bir_lowering=False, num_devices=1)
    arrays, args = {}, []
    given = {n: inputs[n] for n in ("x", "adj", "L1_gnn_W", "L1_gnn_a")}
    given["constants"] = constants()
    for name, value in given.items():
        a = _np.ascontiguousarray(value)
        arrays[f"in_{name}_dram"] = a
        args.append(nc.dram_tensor(f"in_{name}_dram", a.shape, _mybir.dt.from_np(a.dtype), kind="ExternalInput").ap())
    args.append(nc.dram_tensor("out_0_dram", (N, D), _mybir.dt.float32, kind="ExternalOutput").ap())
    args.append(nc.dram_tensor("h_rows", (N, D), _mybir.dt.float32, kind="Internal").ap())
    args.append(nc.dram_tensor("e_rows", (N, ROWLEN), _mybir.dt.float32, kind="Internal").ap())
    build(nc, *args)
    r = _run(nc, [arrays], core_ids=[0])
    return r.results[0]["out_0_dram"]
```

```python
import concourse.bass as bass
from concourse import mybir
from contextlib import ExitStack

F32, I32 = mybir.dt.float32, mybir.dt.int32
BF16, F16 = mybir.dt.bfloat16, mybir.dt.float16
ALU = mybir.AluOpType
ACT = mybir.ActivationFunctionType
AX = mybir.AxisListType.X

P = 128
N = 4096
T = N // P
D = 128
HALF = N // 2
GROUPS = 256
BITS = N // GROUPS
LEVELS = 3
SLOTS = 16
BLOCKS = 5
EDGES = BLOCKS * P
E2 = EDGES + 2
ROWLEN = D + 2
EW = D + 1
NEG_SLOPE = 0.01
EPS = 1e-5
HMAX = 64.0
BIG = 1e30
MASKED = -9e16
PAIRS = T // 2
OFF = 0.375
BASE = OFF * OFF

C_ID, C_TRI, C_ROW1, C_IOTA, C_G = 0, P, 2 * P, 3 * P, 3 * P + EDGES
C_PB = C_G + GROUPS
C_S = C_PB + BLOCKS
C_P1 = C_S + SLOTS
CONSTS = C_P1 + 1


def constants():
    import numpy as np
    c = np.zeros((P, CONSTS), np.float32)
    p = np.arange(P, dtype=np.float32)[:, None]
    c[:, C_ID:C_ID + P] = np.eye(P)
    c[:, C_TRI:C_TRI + P] = np.triu(np.ones((P, P)), 1)
    c[:, C_ROW1:C_ROW1 + P] = np.arange(P)[None] + 1
    c[:, C_IOTA:C_IOTA + EDGES] = np.arange(EDGES)[None]
    c[0, C_G:C_G + GROUPS] = np.arange(GROUPS)
    c[1, C_G:C_G + GROUPS] = -BASE * 2 ** (BITS + 10)
    c[2, C_G:C_G + GROUPS] = BASE * 2 ** 10
    c[:, C_PB:C_PB + BLOCKS] = p + P * np.arange(BLOCKS)[None]
    c[:, C_S:C_S + SLOTS] = np.arange(SLOTS)[None]
    c[:, C_P1:C_P1 + 1] = p + 1
    return c


class Chain:

    def __init__(self, eng, sem):
        self.eng, self.sem, self.n, self.seen = eng, sem, 0, 0
        eng.sem_inc(sem)
        eng.sem_clear(sem)

    def did(self, ins):
        ins.then_inc(self.sem, 1)
        self.n += 1
        return self.n

    def need(self, n):
        if self.seen < n:
            self.eng.wait_ge(self.sem, n)
            self.seen = n

    def then(self, ins):
        self.need(self.did(ins))

    def wait(self):
        self.need(self.n)


def build(nc, x, adj, W, a, consts, out, h_rows, e_rows):
    ctx = ExitStack()
    with ctx:
        def sb(name, shape, dt=F32):
            return ctx.enter_context(nc.sbuf_tensor(name, shape, dt))

        def ps(name, cols):
            return ctx.enter_context(nc.psum_tensor(name, [P, cols], F32))

        def sem(name):
            return ctx.enter_context(nc.semaphore(name))

        cst = sb("cst", [P, CONSTS])
        ident = cst[:, C_ID:C_ID + P]
        row1 = cst[:, C_ROW1:C_ROW1 + P]
        edge_pb = cst[:, C_PB:C_PB + BLOCKS]
        slot_iota = cst[:, C_S:C_S + SLOTS]
        code_w = sb("code_w", [P, BITS, P], BF16)
        key_row = sb("key_row", [P, GROUPS], BF16)
        ones_b = sb("ones_b", [P, P], BF16)
        diag_cap = sb("diag_cap", [P, P], BF16)
        tri = sb("tri", [P, P], F16)
        iota_e = sb("iota_e", [P, EDGES], F16)
        cut_w = sb("cut_w", [P, 2, P], F16)
        adj_in = sb("adj_in", [P, 2, N], I32)
        mask = sb("mask", [P, 2, 2, N], BF16)
        X = sb("X", [P, T, D])
        H = sb("H", [P, T, D])
        EN = sb("EN", [P, T, D + 2])
        G = sb("G", [P, 2, 2, BLOCKS, EW])
        stat6 = sb("stat6", [P, 4, 6])
        mv = sb("mv", [P, T, 2])
        mv1 = sb("mv1", [P, 2, 2])
        std = sb("std", [P, T])
        rstd = sb("rstd", [P, T])
        eps = sb("eps", [P, 1])
        minus_off = sb("minus_off", [P, 1])
        nmr = sb("nmr", [P, T])
        deg = sb("deg", [P, T, 2])
        cnt = sb("cnt", [P, T])
        start = sb("start", [P, T])
        end = sb("end", [P, T])
        rest = sb("rest", [P, T])
        last_row = sb("last_row", [P, T, BLOCKS])
        idx_all = sb("idx_all", [P, T, BLOCKS], I32)
        idx = [sb(f"idx{q}", [P, 2 * BLOCKS], I32) for q in range(2)]
        top = sb("top", [P, 2, SLOTS])
        keys2 = sb("keys2", [P, 2, GROUPS])
        topi = sb("topi", [P, 2, SLOTS], I32)
        grp = sb("grp", [P, 2, SLOTS], I32)
        powr = sb("powr", [P, LEVELS, 2 * SLOTS], I32)
        rem = sb("rem", [P, LEVELS, 2 * SLOTS])
        shf = sb("shf", [P, LEVELS, 2 * SLOTS], I32)
        cand = sb("cand", [P, 2, LEVELS, SLOTS])
        cand2 = sb("cand2", [P, 2, LEVELS * SLOTS])
        val = sb("val", [P, 2, SLOTS])
        valid = sb("valid", [P, 2, SLOTS])
        V = sb("V", [P, 2, 20], F16)
        NV = sb("NV", [P, 2, 20], F16)
        ge_s = sb("ge_s", [P, 2, E2], F16)
        ge_e = sb("ge_e", [P, 2, E2], F16)
        kpos = sb("kpos", [P, 2 * BLOCKS])
        onehot = sb("onehot", [P, 2 * BLOCKS, SLOTS])
        pick = sb("pick", [P, 2 * BLOCKS, SLOTS])
        red = sb("red", [P, 2 * BLOCKS])
        lastm = sb("lastm", [P, 2 * BLOCKS])
        cut = sb("cut", [P, 2, 2, EDGES], BF16)
        scan = sb("scan", [P, EDGES])
        scanT = sb("scanT", [P, 2, BLOCKS, P])
        S = sb("S", [P, 2, BLOCKS, P])
        agg = sb("agg", [P, 2, D])
        h1p = sb("h1p", [P, 2, D])
        h1Tp = sb("h1Tp", [P, 2, P])
        h1, h1T = h1p[:, 0, :], h1Tp[:, 0, :]
        WX = sb("WX", [P, D + 2])
        Wsb = sb("Wsb", [P, D])
        asb = sb("asb", [P, 2])
        late = adj_in[:, :, :].rearrange("p q n -> p (q n)").bitcast(F32)
        late = late[:, 0:12 * EDGES].rearrange("p (k q e) -> p k q e", k=6, q=2)
        z, exp_pos, exp_neg, prob = (late[:, k] for k in range(4))
        probT = late[:, 4].rearrange("p q (b d) -> p q b d", b=BLOCKS)
        off_s, off_e, off = (sb(n, [P, EDGES], BF16) for n in ("off_s", "off_e", "off"))
        zmax = sb("zmax", [P, 1])
        lin = sb("lin", [P, 2])
        neg_max = sb("neg_max", [P, 2])
        bias = sb("bias", [P, 2, 2])
        src01 = sb("src01", [P, T])
        xself = sb("xself", [P, T])
        wself = sb("wself", [P, 2])
        den = sb("den", [P, 2])
        dn = sb("dn", [P, 2])
        num = sb("num", [P, 2, D])
        O = sb("O", [P, 2, D])
        junk = sb("junk", [P, 2 * T])

        bad = sb("bad", [P, 4, T])
        bad_row = sb("bad_row", [P, 1])
        general = sb("general", [P, 1], I32)
        ones = sb("ones", [P, P])
        row_in = adj_in
        hT = EN[:, :, :].rearrange("p t d -> p (t d)")[:, 0:N]
        wide = mask[:, 0, :, :].rearrange("p u n -> p (u n)").bitcast(F32)
        e_wide = adj_in[:, 1, :].bitcast(F32)
        t_all = H[:, :, :].rearrange("p t d -> p (t d)")
        aggT = h1T

        front_ps = ps("front_ps", 1024)
        key_ps = front_ps[:, 0:512]
        emb_ps = front_ps[:, 512:1024]
        list_ps = ps("list_ps", 512)
        gt_ps = ps("gt_ps", 1024)
        back_ps = ps("back_ps", 1024)
        seg_ps = ps("seg_ps", 512)
        LB = list_ps[:, 8:8 + 40 * BLOCKS].rearrange("p (b v) -> p b v", v=20)
        tb_ps = [back_ps, front_ps]
        seg2 = seg_ps[:, 0:2 * D].rearrange("p (u d) -> p u d", u=2)

        cst_in, x_in, w_in = sem("cst_in"), [sem(f"x_in{c}") for c in range(4)], sem("w_in")
        cst_made = sem("cst_made")
        adj_loaded = [[sem(f"adj_loaded{q}{h}") for h in range(2)] for q in range(2)]
        signed = sem("signed")
        diag_cleared = sem("diag_cleared")
        keys_made, keys_taken = sem("keys_made"), sem("keys_taken")
        counted, start_made, spans_made = sem("counted"), sem("start_made"), sem("spans_made")
        lists_made, lists_taken = sem("lists_made"), sem("lists_taken")
        idx_ready = sem("idx_ready")
        cut_made, cut_saved = sem("cut_made"), sem("cut_saved")
        gathered = [[sem(f"gathered{q}_{b}") for b in range(2 * BLOCKS)] for q in range(2)]
        gt_made, scanned = sem("gt_made"), sem("scanned")
        back_made, back_saved = sem("back_made"), sem("back_saved")
        ends_made, seg_made, seg_taken = sem("ends_made"), sem("seg_made"), sem("seg_taken")
        x1_stats, std1_made, rstd1_made, h1_made, h1T_made, h1T_saved = (sem("x1_stats"), sem("std1_made"), sem("rstd1_made"), sem("h1_made"), sem("h1T_made"), sem("h1T_saved"))
        emb_made, emb_saved, emb_stored = sem("emb_made"), sem("emb_saved"), [sem("emb_stored0"), sem("emb_stored1")]
        std0_made = sem("std0_made")
        stats0, h0_made, h0_stored = sem("stats0"), sem("h0_made"), sem("h0_stored")
        wx_ps_made, wx_saved = sem("wx_ps_made"), sem("wx_saved")
        c_ln, c_set, c_keys, c_span, c_list, c_seg = (sem(n) for n in ("c_ln", "c_set", "c_keys", "c_span", "c_list", "c_seg"))
        idx2_ready, tb_made, z_made, m_made = sem("idx2_ready"), sem("tb_made"), sem("z_made"), sem("m_made")
        c_z, c_fin = sem("c_z"), sem("c_fin")
        prob_made, probT_made, probT_saved, num_made, num_taken = (sem(n) for n in ("prob_made", "probT_made", "probT_saved", "num_made", "num_taken"))
        scales0, idx_kept, probs_made = sem("scales0"), sem("idx_kept"), sem("probs_made")
        self_made, exps_made = sem("self_made"), sem("exps_made")
        out_made, out_stored = sem("out_made"), [sem("out_stored0"), sem("out_stored1")]

        passed = {"pool": sem("pool_passed"), "dve": sem("dve_passed")}

        def settled(eng, who):
            eng.sem_inc(passed[who])

        checked, bad_summed, flag_made = sem("checked"), sem("bad_summed"), sem("flag_made")
        gx_in, gh_ready, ghT_ps = sem("gx_in"), sem("gh_ready"), sem("ghT_ps")
        grow_in = [sem("grow_in0"), sem("grow_in1")]
        grow_used, gmax_made, gagg_made, gagg_taken = sem("grow_used"), sem("gmax_made"), sem("gagg_made"), sem("gagg_taken")
        c_gen = sem("c_gen")
        gvar_made, gstd_made, gh1_made, gh1T_ps, gh1T_saved = (sem(n) for n in ("gvar_made", "gstd_made", "gh1_made", "gh1T_ps", "gh1T_saved"))
        gemb_ps, gt_ps_made = sem("gemb_ps"), sem("gt_ps_made")
        gadj_in, gadj_used, gmax1_made, gprob_made = (sem(n) for n in ("gadj_in", "gadj_used", "gmax1_made", "gprob_made"))
        gt_ready, gprob_ready = sem("gt_ready"), sem("gprob_ready")
        gprobT_ps, gprobT_saved, gnum_made, gout_made, gout_stored = (sem(n) for n in ("gprobT_ps", "gprobT_saved", "gnum_made", "gout_made", "gout_stored"))

        block = ctx.enter_context(nc.Block())

        x_v = x.rearrange("(t p) d -> p t d", p=P)
        out_v = out.rearrange("(t p) d -> p t d", p=P)
        h_v = h_rows.rearrange("(t p) d -> p t d", p=P)
        e_v = e_rows.rearrange("(t p) d -> p t d", p=P)
        adj_v = adj.rearrange("(t p) n -> p t n", p=P)

        def wait(eng, s, value):
            if isinstance(value, int) and value <= 0:
                return
            eng.wait_ge(s, value)

        def steps(eng, step, last, lead, ahead):
            hi = PAIRS - ahead
            hi -= (hi - lead) % 2
            for i in range(lead):
                step(i, i % 2)
            with eng.Fori(0, (hi - lead) // 2) as turn:
                for u in range(2):
                    step(turn * 2 + (lead + u), (lead + u) % 2)
            for i in range(hi, last):
                step(i, i % 2)

        def within(i, off):
            return not isinstance(i, int) or 0 <= i + off < PAIRS

        def pair(buf, i, cols=slice(None)):
            return buf[:, bass.ds(i * 2, 2), cols] if len(buf.shape) == 3 else buf[:, bass.ds(i * 2, 2)]

        XC = 4
        TC = T // XC

        def flag(eng):
            eng.wait_ge(flag_made, 1)
            return eng.value_load(general[0:1, 0:1], min_val=0, max_val=1 << 20)

        def tile(buf, t, cols=slice(None)):
            return buf[:, bass.ds(t, 1), cols].rearrange("p a d -> p (a d)")

        @block.sync
        def _(sp):
            sp.dma_start(cst[:, :], consts).then_inc(cst_in, 16)
            for c in range(XC):
                sp.dma_start(X[:, c * TC:(c + 1) * TC, :], x_v[:, c * TC:(c + 1) * TC, :]).then_inc(x_in[c], 16)
            sp.dma_start(Wsb[:, :], W).then_inc(w_in, 16)
            for h in range(2):
                sp.dma_start(asb[:, h:h + 1], a[h * P:(h + 1) * P, :]).then_inc(w_in, 16)

            def load(i):
                for u in range(2):
                    t = i * 2 + u
                    for h in range(2):
                        wait(sp, signed, (t - 2) * 2 + h + 1)
                        sp.dma_start(adj_in[:, u, h * HALF:(h + 1) * HALF],
                                     tile(adj_v, t, slice(h * HALF, (h + 1) * HALF))).then_inc(adj_loaded[u][h], 16)

            load(0)
            load(1)
            for c in range(XC):
                sp.wait_ge(h0_made, (c + 1) * TC)
                sp.dma_start(h_v[:, c * TC:(c + 1) * TC, :], H[:, c * TC:(c + 1) * TC, :]).then_inc(h0_stored, 16)

            def step(i, q):
                if within(i, 2):
                    load(i + 2)
                if within(i, -4):
                    sp.wait_ge(emb_saved, i - 3)
                    sp.dma_start(pair(e_v, i - 4), pair(EN, i - 4)).then_inc(emb_stored[q], 16)
            steps(sp, step, PAIRS + 4, 4, 2)

            with sp.Fori(0, PAIRS) as i:
                for u in range(2):
                    sp.wait_ge(out_made, i * 2 + u + 1)
                    sp.dma_start(tile(out_v, i * 2 + u), O[:, u, :]).then_inc(out_stored[u], 16)
            for q in range(2):
                sp.wait_ge(out_stored[q], 16 * T // 2)

            with sp.If(flag(sp) > 0):
                sp.dma_start(X[:, :, :], x_v).then_inc(gx_in, 16)
                with sp.Fori(0, N // 2) as duo:
                    sp.wait_ge(grow_used, duo * 2 + 1)
                    for u in range(2):
                        sp.dma_start(row_in[:, u, :], adj[bass.ds(duo * 2 + u, 1), :].broadcast_to([P, N])).then_inc(grow_in[u], 16)
                with sp.Fori(0, T) as t:
                    sp.wait_ge(gadj_used, t + 1)
                    sp.dma_start(row_in[:, 0, :], tile(adj_v, t)).then_inc(gadj_in, 16)
                    sp.wait_ge(gout_made, t + 1)
                    sp.dma_start(tile(out_v, t), O[:, 0, :]).then_inc(gout_stored, 16)
                sp.wait_ge(gout_stored, 16 * T + 16)

        @block.gpsimd
        def _(pool):
            pool.wait_ge(h0_stored, 16 * XC)

            def gather(table, width, q, u):
                for b in range(BLOCKS):
                    k = u * BLOCKS + b
                    pool.indirect_dma_start(out=G[:, q, u, b, 0:width], out_offset=None, in_=table,
                                            in_offset=bass.IndirectOffsetOnAxis(ap=idx[q][:, k:k + 1], axis=0)).then_inc(gathered[q][k], 16)

            def step(i, q):
                pool.wait_ge(idx_ready, i + 1)
                for u in range(2):
                    wait(pool, gt_made, i * 2 + u - 3)
                    settled(pool, "pool")
                    gather(h_rows, D, q, u)
            steps(pool, step, PAIRS, 2, 0)
            for q in range(2):
                pool.wait_ge(emb_stored[q], 16 * PAIRS // 2)

            def step1(i, q):
                pool.wait_ge(idx2_ready, i + 1)
                for u in range(2):
                    wait(pool, num_made, i * 2 + u - 3)
                    settled(pool, "pool")
                    gather(e_rows, EW, q, u)
            steps(pool, step1, PAIRS, 2, 0)

        @block.scalar
        def _(act):
            def square(i, q, u, h):
                t = i * 2 + u
                act.wait_ge(adj_loaded[u][h], i * 16 + 16)
                wait(act, keys_made, t - 3)
                act.activation(mask[:, q, u, h * HALF:(h + 1) * HALF], adj_in[:, u, h * HALF:(h + 1) * HALF], ACT.Square,
                               bias=minus_off[:, :], accum_out=tile(deg, t, slice(h, h + 1))).then_inc(signed, 1)

            act.wait_ge(cst_made, 1)
            for c in range(XC):
                ts = slice(c * TC, (c + 1) * TC)
                act.wait_ge(stats0, c + 1)
                act.activation(std[:, ts], mv[:, ts, 1], ACT.Sqrt, bias=eps[:, :]).then_inc(std0_made, 1)
                act.wait_ge(scales0, c + 1)
                for t in range(c * TC, (c + 1) * TC):
                    act.activation(H[:, t, :], X[:, t, :], ACT.Relu, bias=nmr[:, t:t + 1], scale=rstd[:, t:t + 1]).then_inc(h0_made, 1)
                if c > 0 and c < 3:
                    square(0, 0, 0, c - 1)
            square(0, 0, 1, 0)
            square(0, 0, 1, 1)
            act.wait_ge(wx_ps_made, 1)
            act.activation(WX[:, :], emb_ps[:, 0:D + 2], ACT.Copy).then_inc(wx_saved, 1)
            for u in range(2):
                for h in range(2):
                    square(1, 1, u, h)

            def save_scan(i, u):
                act.wait_ge(back_made, i * 2 + u + 1)
                wait(act, seg_made, i * 2 + u - 1)
                act.activation(scanT[:, u, :, :].rearrange("p b d -> p (b d)"), back_ps[:, 0:EDGES], ACT.Copy).then_inc(back_saved, 1)

            def save_cut(i, q, u):
                act.wait_ge(cut_made, i * 2 + u + 1)
                wait(act, scanned, i * 2 + u - 3)
                act.activation(cut[:, q, u, :], back_ps[:, 0:EDGES], ACT.Copy).then_inc(cut_saved, 1)

            def step(i, q):
                if within(i, -3):
                    e = i - 3
                    act.wait_ge(h1T_made, e + 1)
                    wait(act, emb_made, e)
                    act.activation(h1Tp[:, :, :].rearrange("p u d -> p (u d)"), emb_ps[:, 0:2 * P], ACT.Copy).then_inc(h1T_saved, 1)
                if within(i, 2):
                    square(i + 2, q, 0, 0)
                    square(i + 2, q, 0, 1)
                if within(i, -2):
                    save_scan(i - 2, 0)
                if within(i, -3):
                    act.wait_ge(emb_made, e + 1)
                    act.wait_ge(rstd1_made, e + 1)
                    for u in range(2):
                        ins = act.activation(tile(EN, e * 2 + u), emb_ps[:, u * (D + 2):(u + 1) * (D + 2)], ACT.Copy,
                                             scale=rstd[:, bass.ds(e * 2 + u, 1)])
                    ins.then_inc(emb_saved, 1)
                if within(i, 2):
                    square(i + 2, q, 1, 0)
                if within(i, -2):
                    save_scan(i - 2, 1)
                if within(i, 2):
                    square(i + 2, q, 1, 1)
                if within(i, 0):
                    save_cut(i, q, 0)
                    save_cut(i, q, 1)
                if within(i, -2):
                    r = i - 2
                    act.wait_ge(x1_stats, r + 1)
                    act.activation(pair(std, r), mv1[:, :, 1], ACT.Sqrt, bias=eps[:, :]).then_inc(std1_made, 1)
                    wait(act, h1T_made, r)
                    for u in range(2):
                        ins = act.activation(h1p[:, u, :], tile(X, r * 2 + u), ACT.Relu, bias=nmr[:, bass.ds(r * 2 + u, 1)])
                    ins.then_inc(h1_made, 1)
            steps(act, step, PAIRS + 3, 4, 2)

            def tile1(t, u):
                if not isinstance(t, int) or t >= 1:
                    act.wait_ge(probT_made, t)
                    wait(act, num_made, t - 2)
                    act.activation(probT[:, 1 - u, :, :].rearrange("p b d -> p (b d)"), gt_ps[:, 0:EDGES], ACT.Copy).then_inc(probT_saved, 1)
                if not isinstance(t, int) or t < T:
                    act.wait_ge(m_made, t + 1)
                    wait(act, probs_made, t - 1)
                    act.activation(exp_pos[:, u, :], z[:, u, :], ACT.Exp, bias=bias[:, u, 0:1])
                    act.activation(exp_neg[:, u, :], z[:, u, :], ACT.Exp, bias=bias[:, u, 1:2], scale=NEG_SLOPE)
                    wait(act, out_made, t - 1)
                    act.activation(wself[:, u:u + 1], xself[:, bass.ds(t, 1)], ACT.Exp, bias=neg_max[:, u:u + 1]).then_inc(exps_made, 1)

            act.wait_ge(self_made, 1)

            def step1(i, q):
                for u in range(2):
                    tile1(i * 2 + u, u)
            steps(act, step1, PAIRS, 2, 0)
            tile1(T, 0)

            with act.If(flag(act) > 0):
                with act.Fori(0, T) as t:
                    act.wait_ge(gvar_made, t + 1)
                    act.activation(std[:, bass.ds(t, 1)], mv1[:, 0, 1:2], ACT.Sqrt, bias=eps[:, :]).then_inc(gstd_made, 1)
                    act.activation(h1, tile(X, t), ACT.Relu, bias=nmr[:, bass.ds(t, 1)]).then_inc(gh1_made, 1)
                    act.wait_ge(gh1T_ps, t + 1)
                    act.activation(h1T, emb_ps[:, 0:P], ACT.Copy).then_inc(gh1T_saved, 1)
                with act.Fori(0, T) as t:
                    act.wait_ge(gmax1_made, t + 1)
                    act.activation(e_wide, e_wide, ACT.Exp, bias=neg_max[:, 0:1], accum_out=den[:, 0:1]).then_inc(gprob_made, 1)

        @block.vector
        def _(dve):
            dve.wait_ge(cst_in, 16)
            for k in range(BITS):
                dve.tensor_scalar(code_w[:, k, :], ident, float(2 ** (k + 10)), None, ALU.mult)
            dve.tensor_copy(key_row[:, :], cst[:, C_G:C_G + GROUPS])
            dve.tensor_scalar(diag_cap[:, :], ident, -4096.0, 4096.0 + BASE, ALU.mult, ALU.add)
            dve.memset(ones_b[:, :], 1.0)
            dve.memset(minus_off[:, :], -OFF)
            dve.memset(ge_s[:, :, 0:2], 0.0)
            dve.memset(ones[:, :], 1.0)
            dve.tensor_copy(tri[:, :], cst[:, C_TRI:C_TRI + P])
            dve.tensor_copy(iota_e[:, :], cst[:, C_IOTA:C_IOTA + EDGES])
            for u in range(2):
                dve.tensor_copy(V[:, u, 17:18], cst[:, C_P1:C_P1 + 1])
            dve.memset(cut_w[:, 1, :], HMAX)
            dve.memset(eps[:, :], EPS)
            dve.memset(cut_w[:, 0, :], -HMAX).then_inc(cst_made, 1)
            dve.wait_ge(cst_made, 1)

            def means(link, t):
                at = t % 4
                done = [link.did(dve.bn_stats(stat6[:, at + u, :], X[:, t + u, :])) for u in range(2)]
                for u in range(2):
                    link.need(done[u])
                    link.did(dve.bn_aggr(mv[:, t + u, :], stat6[:, at + u, :]))

            link = Chain(dve, c_ln)

            def scales(c):
                ts = slice(c * TC, (c + 1) * TC)
                dve.wait_ge(std0_made, c + 1)
                link.then(dve.reciprocal(rstd[:, ts], std[:, ts]))
                dve.scalar_tensor_tensor(nmr[:, ts], mv[:, ts, 0], -1.0, rstd[:, ts], ALU.mult, ALU.mult).then_inc(scales0, 1)

            for c in range(XC):
                dve.wait_ge(x_in[c], 16)
                for t in range(c * TC, (c + 1) * TC, 2):
                    means(link, t)
                link.wait()
                dve.sem_inc(stats0)
                if c > 0:
                    scales(c - 1)
            scales(XC - 1)

            def clear_diagonal(i, q, u):
                dve.wait_ge(signed, i * 4 + u * 2 + 2)
                blk = mask[:, q, u, bass.ds((i * 2 + u) * P, P)]
                dve.tensor_tensor(blk, blk, diag_cap[:, :], ALU.min).then_inc(diag_cleared, 1)

            def scan_max(i, q, u):
                dve.wait_ge(gt_made, i * 2 + u + 1)
                dve.wait_ge(cut_saved, i * 2 + u + 1)
                wait(dve, back_made, i * 2 + u)
                dve.tensor_tensor_scan(scan[:, :], cut[:, q, u, :], gt_ps[:, 0:EDGES], 0.0, ALU.add, ALU.max).then_inc(scanned, 1)

            def row_ends(i, u, blocks):
                for b in blocks:
                    ins = dve.tensor_scalar(S[:, u, b, :], row1, tile(last_row, i * 2 + u, slice(b, b + 1)), None, ALU.is_equal)
                if b == BLOCKS - 1:
                    ins.then_inc(ends_made, 1)

            def read_keys(i, prev, q):
                fill = within(i, -2)
                take = within(i, 0)
                if take:
                    dve.wait_ge(keys_made, i * 2 + 2)
                    link = Chain(dve, c_keys)
                    keys = [key_ps[:, u * GROUPS:(u + 1) * GROUPS] for u in range(2)]
                    m = [link.did(dve.max(top[:, u, 0:8], keys[u])) for u in range(2)]
                    link.need(m[0])
                    m[0] = link.did(dve.match_replace(keys2[:, 0, :], top[:, 0, 0:8], keys[0], -1.0))
                    link.need(m[1])
                    m[1] = link.did(dve.match_replace(keys2[:, 1, :], top[:, 1, 0:8], keys[1], -1.0))
                    link.need(m[0])
                    link.did(dve.max(top[:, 0, 8:16], keys2[:, 0, :]))
                    link.need(m[1])
                    dve.sem_inc(keys_taken)
                    m = link.did(dve.max(top[:, 1, 8:16], keys2[:, 1, :]))
                if fill:
                    wait(dve, seg_made, prev * 2)
                    scan_max(prev, q, 0)
                if take:
                    link.need(m)
                    link.did(dve.tensor_copy(topi[:, :, :], top[:, :, :]))
                    left = top[:, :, :].rearrange("p u s -> p (u s)")
                for v in range(LEVELS):
                    if take:
                        link.wait()
                        link.did(dve.tensor_scalar(powr[:, v, :], left.bitcast(I32), 0x7F800000, None, ALU.bitwise_and))
                    if fill:
                        row_ends(prev, 0, ((0,), (2,), (4,))[v])
                    if take:
                        link.wait()
                        link.did(dve.tensor_tensor(rem[:, v, :], left, powr[:, v, :].bitcast(F32), ALU.subtract))
                        left = rem[:, v, :]
                    if fill:
                        if v < 2:
                            row_ends(prev, 0, ((1,), (3,))[v])
                        else:
                            scan_max(prev, q, 1)
                if take:
                    link.did(dve.tensor_scalar(grp[:, :, :], topi[:, :, :], GROUPS - 1, None, ALU.bitwise_and))
                    m = link.did(dve.tensor_scalar(shf[:, :, :], powr[:, :, :], 15, None, ALU.logical_shift_right))
                    link.need(m - 2)
                    link.did(dve.tensor_reduce(pair(rest, i), rem[:, LEVELS - 1, :].rearrange("p (u s) -> p u s", u=2), AX, ALU.max))
                    link.need(m)
                    m = []
                    for u in range(2):
                        m.append(link.did(dve.scalar_tensor_tensor(
                            cand[:, u, :, :], shf[:, :, u * SLOTS:(u + 1) * SLOTS], float(1 - (127 + 8) * GROUPS),
                            grp[:, u:u + 1, :].broadcast_to([P, LEVELS, SLOTS]), ALU.add, ALU.add)))
                    cands = [cand[:, u, :, :].rearrange("p v s -> p (v s)") for u in range(2)]
                    for u in range(2):
                        link.need(m[u])
                        m[u] = link.did(dve.max(val[:, u, 0:8], cands[u]))
                if fill:
                    row_ends(prev, 1, (0,))
                if take:
                    for u in range(2):
                        link.need(m[u])
                        m[u] = link.did(dve.match_replace(cand2[:, u, :], val[:, u, 0:8], cands[u], -1.0))
                if fill:
                    row_ends(prev, 1, (1,))
                if take:
                    for u in range(2):
                        link.need(m[u])
                        m[u] = link.did(dve.max(val[:, u, 8:16], cand2[:, u, :]))
                if fill:
                    row_ends(prev, 1, (2,))
                if take:
                    link.wait()
                    m = link.did(dve.tensor_scalar(valid[:, :, :], val[:, :, :], 0.0, None, ALU.is_gt))
                    link.did(dve.tensor_scalar(V[:, :, 0:SLOTS], val[:, :, :], 1.0, -float(N // 2 + 1), ALU.max, ALU.add))
                    link.need(m)
                    link.did(dve.tensor_reduce(pair(cnt, i), valid[:, :, :], AX, ALU.add))
                if fill:
                    row_ends(prev, 1, (3,))
                if take:
                    link.wait()
                    dve.tensor_copy(V[:, :, 18], pair(cnt, i)).then_inc(counted, 1)
                if fill:
                    row_ends(prev, 1, (4,))

            def spans(i):
                dve.wait_ge(start_made, i + 1)
                wait(dve, cut_made, i * 2)
                link = Chain(dve, c_span)
                a = link.did(dve.tensor_copy(pair(start, i), list_ps[:, 0:2]))
                b = link.did(dve.tensor_copy(V[:, :, 16], list_ps[:, 0:2]))
                c = link.did(dve.tensor_tensor(pair(end, i), list_ps[:, 0:2], pair(cnt, i), ALU.add))
                link.need(a)
                for u in range(2):
                    link.did(dve.tensor_scalar(ge_s[:, u, 2:E2], iota_e[:, :], start[:, bass.ds(i * 2 + u, 1)], None, ALU.is_ge))
                link.need(b)
                link.did(dve.tensor_scalar(NV[:, :, 0:19], V[:, :, 0:19], -1.0, None, ALU.mult))
                link.need(c)
                for u in range(2):
                    ins = dve.tensor_scalar(ge_e[:, u, 2:E2], iota_e[:, :], end[:, bass.ds(i * 2 + u, 1)], None, ALU.is_ge)
                    if u == 0:
                        link.did(ins)
                link.wait()
                ins.then_inc(spans_made, 1)

            def lists_and_residual(i, r, q):
                take, fill = within(i, 0), within(i, -2)
                if fill:
                    dve.wait_ge(seg_made, r * 2 + 2)
                    dve.tensor_tensor(agg[:, :, :], seg2, pair(H, r), ALU.max).then_inc(seg_taken, 1)
                    wait(dve, std1_made, r)
                if take:
                    dve.wait_ge(lists_made, i + 1)
                    a = Chain(dve, c_list)
                    over_slots = lambda v: v.rearrange("p (b s) -> p b s", s=1).broadcast_to([P, 2 * BLOCKS, SLOTS])
                    a.did(dve.tensor_tensor(kpos[:, :].rearrange("p (u b) -> p u b", u=2),
                                            edge_pb.rearrange("p (u b) -> p u b", u=1).broadcast_to([P, 2, BLOCKS]),
                                            LB[:, :, 16].rearrange("p (u b) -> p u b", u=2), ALU.subtract))
                if fill:
                    dve.wait_ge(seg_taken, r + 1)
                    b = Chain(dve, c_seg)
                    b.did(dve.tensor_tensor(pair(X, r), pair(X, r), agg[:, :, :], ALU.add))
                if take:
                    a.wait()
                    a.did(dve.tensor_tensor(onehot[:, :, :], slot_iota.rearrange("p (b s) -> p b s", b=1).broadcast_to([P, 2 * BLOCKS, SLOTS]),
                                            over_slots(kpos[:, :]), ALU.is_equal))
                if fill:
                    b.wait()
                    m = [b.did(dve.bn_stats(stat6[:, 0, :], tile(X, r * 2)))]
                if take:
                    a.wait()
                    a.did(dve.tensor_tensor(pick[:, :, :], onehot[:, :, :], LB[:, :, 0:SLOTS], ALU.mult))
                    k = a.did(dve.scalar_tensor_tensor(lastm[:, :], kpos[:, :], 1.0, LB[:, :, 18], ALU.add, ALU.is_equal))
                if fill:
                    m.append(b.did(dve.bn_stats(stat6[:, 1, :], tile(X, r * 2 + 1))))
                if take:
                    a.need(k)
                    k = a.did(dve.tensor_reduce(red[:, :], pick[:, :, :], AX, ALU.add))
                    dve.tensor_tensor(pair(last_row, i).rearrange("p a b -> p (a b)"), lastm[:, :], LB[:, :, 17], ALU.mult).then_inc(lists_taken, 1)
                if fill:
                    for u in range(2):
                        b.need(m[u])
                        b.did(dve.bn_aggr(mv1[:, u, :], stat6[:, u, :]))
                if take:
                    a.need(k)
                    dve.tensor_scalar(idx[q][:, :], red[:, :], float(N // 2), float(N - 1), ALU.add, ALU.min).then_inc(idx_ready, 1)
                    dve.tensor_scalar(pair(idx_all, i).rearrange("p a b -> p (a b)"), red[:, :], float(N // 2), float(N - 1), ALU.add, ALU.min).then_inc(idx_kept, 1)
                if fill:
                    b.wait()
                    dve.tensor_scalar(pair(nmr, r), mv1[:, :, 0], -1.0, None, ALU.mult).then_inc(x1_stats, 1)

            def inverse_std(i):
                dve.wait_ge(std1_made, i + 1)
                dve.reciprocal(pair(rstd, i), pair(std, i)).then_inc(rstd1_made, 1)

            clear_diagonal(0, 0, 0)
            clear_diagonal(0, 0, 1)

            def step(i, q):
                read_keys(i, i - 2, q)
                if isinstance(i, int) and i == 0:
                    clear_diagonal(1, 1, 0)
                    clear_diagonal(1, 1, 1)
                if within(i, 0):
                    spans(i)
                if within(i, 2):
                    clear_diagonal(i + 2, q, 0)
                    clear_diagonal(i + 2, q, 1)
                lists_and_residual(i, i - 2, q)
                if within(i, -2):
                    inverse_std(i - 2)
            steps(dve, step, PAIRS + 2, 2, 2)

            link = Chain(dve, c_set)
            dve.wait_ge(signed, 2 * T)
            link.then(dve.tensor_tensor(bad[:, 0, :], deg[:, :, 0], deg[:, :, 1], ALU.add))
            link.then(dve.scalar_tensor_tensor(bad[:, 0, :], cnt[:, :], -0.25, bad[:, 0, :], ALU.mult, ALU.add))
            link.then(dve.tensor_scalar(bad[:, 0, :], bad[:, 0, :], -(N * BASE + 0.25), None, ALU.add))
            link.then(dve.tensor_tensor(bad[:, 0, :], bad[:, 0, :], bad[:, 0, :], ALU.mult))
            link.did(dve.tensor_scalar(bad[:, 0, :], bad[:, 0, :], 0.01, None, ALU.is_ge))
            link.did(dve.tensor_scalar(bad[:, 1, :], cnt[:, :], float(SLOTS), None, ALU.is_ge))
            link.did(dve.tensor_scalar(bad[:, 2, :], rest[:, :], float(GROUPS), None, ALU.is_ge))
            link.then(dve.tensor_scalar(bad[:, 3, :], end[:, :], float(EDGES), None, ALU.is_gt))
            dve.tensor_reduce(bad_row[:, :], bad[:, :, :].rearrange("p c t -> p (c t)"), AX, ALU.add).then_inc(checked, 1)
            dve.wait_ge(bad_summed, 1)
            dve.tensor_copy(general[:, :], list_ps[:, 0:1]).then_inc(flag_made, 1)

            def copy_idx(i, q):
                wait(dve, tb_made, i * 2 - 2)
                dve.tensor_copy(idx[q][:, :], pair(idx_all, i).rearrange("p a b -> p (a b)")).then_inc(idx2_ready, 1)

            dve.wait_ge(idx_kept, PAIRS)
            copy_idx(0, 0)
            copy_idx(1, 1)
            dve.wait_ge(emb_saved, PAIRS)
            tgt, src = EN[:, :, D], EN[:, :, D + 1]
            link = Chain(dve, c_set)
            link.did(dve.tensor_scalar(src01[:, :], src, NEG_SLOPE, None, ALU.mult))
            link.then(dve.tensor_tensor(junk[:, 0:T], tgt, src, ALU.add))
            dve.scalar_tensor_tensor(xself[:, :], junk[:, 0:T], NEG_SLOPE, junk[:, 0:T], ALU.mult, ALU.max).then_inc(self_made, 1)

            def off_part(link, t, part):
                if isinstance(t, int) and t >= T:
                    return
                if part == 0:
                    link.did(dve.tensor_scalar(off_s[:, :], iota_e[:, :], start[:, bass.ds(t, 1)], -BIG, ALU.is_lt, ALU.mult))
                if part == 1:
                    link.did(dve.tensor_scalar(off_e[:, :], iota_e[:, :], end[:, bass.ds(t, 1)], -BIG, ALU.is_ge, ALU.mult))
                if part == 2:
                    link.did(dve.tensor_tensor(off[:, :], off_s[:, :], off_e[:, :], ALU.add))

            def tile1(t, u):
                has = not isinstance(t, int)
                now, p, f = has or t < T, has or 1 <= t <= T, has or 2 <= t
                tt = bass.ds(t, 1)
                if p:
                    dve.wait_ge(exps_made, t)
                    wait(dve, probT_made, t - 2)
                    dve.scalar_tensor_tensor(prob[:, 1 - u, :], exp_pos[:, 1 - u, :], 0.0, exp_neg[:, 1 - u, :], ALU.max, ALU.max,
                                             accum_out=den[:, 1 - u:2 - u]).then_inc(probs_made, 1)
                if now:
                    dve.wait_ge(tb_made, t + 1)
                link = Chain(dve, c_z)
                if now:
                    k = link.did(dve.tensor_tensor_reduce(z[:, u, :], off[:, :], tb_ps[u][:, 0:EDGES], 1.0, -3e38, ALU.add, ALU.max, zmax[:, :]))
                    link.need(k)
                    dve.sem_inc(z_made)
                    k = link.did(dve.tensor_scalar(lin[:, 0:1], zmax[:, :], tile(EN, t, slice(D + 1, D + 2)), None, ALU.add))
                if f:
                    g = t - 2
                    dve.wait_ge(num_made, t - 1)
                    d = link.did(dve.tensor_tensor(dn[:, 0:1], den[:, u:u + 1], wself[:, u:u + 1], ALU.add))
                    dve.scalar_tensor_tensor(num[:, 0, :], tile(EN, g, slice(0, D)), wself[:, u:u + 1],
                                             seg_ps[:, 0:D], ALU.mult, ALU.add).then_inc(num_taken, 1)
                if now:
                    link.need(k)
                    k = link.did(dve.scalar_tensor_tensor(lin[:, 1:2], lin[:, 0:1], NEG_SLOPE, lin[:, 0:1], ALU.mult, ALU.max))
                if now:
                    off_part(link, t + 1, 0)
                if now:
                    link.need(k)
                    k = link.did(dve.tensor_scalar(neg_max[:, u:u + 1], lin[:, 1:2], xself[:, tt], -1.0, ALU.max, ALU.mult))
                if f:
                    link.need(d)
                    link.did(dve.reciprocal(dn[:, 1:2], dn[:, 0:1]))
                if now:
                    link.need(k)
                    dve.tensor_tensor(bias[:, u, 0:1], neg_max[:, u:u + 1], tile(EN, t, slice(D + 1, D + 2)), ALU.add)
                    dve.tensor_tensor(bias[:, u, 1:2], neg_max[:, u:u + 1], src01[:, tt], ALU.add).then_inc(m_made, 1)
                if f:
                    link.wait()
                    dve.wait_ge(num_taken, t - 1)
                    link.did(dve.tensor_scalar(num[:, 1, :], num[:, 0, :], dn[:, 1:2], 0.0, ALU.mult, ALU.max))
                if now:
                    off_part(link, t + 1, 1)
                if f:
                    link.wait()
                    if has or g >= 2:
                        dve.wait_ge(out_stored[u], (g - u) * 8)
                    dve.tensor_tensor(O[:, u, :], num[:, 1, :], tile(X, g), ALU.add).then_inc(out_made, 1)
                if now:
                    link.wait()
                    off_part(link, t + 1, 2)
                link.wait()

            link = Chain(dve, c_z)
            for part in range(3):
                link.wait()
                off_part(link, 0, part)
            link.wait()

            def step1(i, q):
                tile1(i * 2, 0)
                tile1(i * 2 + 1, 1)
                if within(i, 2) and not (isinstance(i, int) and i + 2 >= PAIRS):
                    copy_idx(i + 2, q)
            steps(dve, step1, PAIRS, 3, 2)
            tile1(T, 0)
            tile1(T + 1, 1)

            with dve.If(flag(dve) > 0):
                dve.sem_inc(grow_used)
                dve.sem_inc(gout_stored, 16)
                with dve.Fori(0, T) as t:
                    link = Chain(dve, c_gen)
                    link.then(dve.tensor_copy(h1, tile(H, t)))
                    dve.sem_inc(gh_ready)
                    dve.wait_ge(ghT_ps, t + 1)
                    link.then(dve.tensor_copy(hT[:, bass.ds(t * P, P)], emb_ps[:, 0:P]))
                dve.wait_ge(gx_in, 16)
                with dve.Fori(0, T) as t:
                    with dve.Fori(0, P // 2) as duo:
                        for u in range(2):
                            dve.wait_ge(grow_in[u], (t * (P // 2) + duo) * 16 + 16)
                            link = Chain(dve, c_gen)
                            link.then(dve.scalar_tensor_tensor(wide, row_in[:, u, :], 0.0, hT, ALU.not_equal, ALU.mult))
                            dve.sem_inc(grow_used)
                            link.then(dve.tensor_reduce(aggT[:, bass.ds(duo * 2 + u, 1)], wide, AX, ALU.max))
                    dve.sem_inc(gmax_made)
                    dve.wait_ge(gagg_made, t + 1)
                    link = Chain(dve, c_gen)
                    link.then(dve.tensor_tensor(tile(X, t), tile(X, t), seg_ps[:, 0:D], ALU.add))
                    dve.sem_inc(gagg_taken)
                with dve.Fori(0, T) as t:
                    link = Chain(dve, c_gen)
                    link.then(dve.bn_stats(stat6[:, 0, :], tile(X, t)))
                    link.then(dve.bn_aggr(mv1[:, 0, :], stat6[:, 0, :]))
                    link.then(dve.tensor_scalar(nmr[:, bass.ds(t, 1)], mv1[:, 0, 0:1], -1.0, None, ALU.mult))
                    dve.sem_inc(gvar_made)
                    dve.wait_ge(gstd_made, t + 1)
                    link.then(dve.reciprocal(rstd[:, bass.ds(t, 1)], std[:, bass.ds(t, 1)]))
                    dve.wait_ge(gemb_ps, t + 1)
                    link.then(dve.tensor_scalar(tile(EN, t), emb_ps[:, P:P + D + 2], rstd[:, bass.ds(t, 1)], None, ALU.mult))
                    link.then(dve.tensor_copy(zmax[:, :], tile(EN, t, slice(D, D + 1))))
                    dve.sem_inc(gt_ready)
                    dve.wait_ge(gt_ps_made, t + 1)
                    link.then(dve.tensor_copy(t_all[:, bass.ds(t * P, P)], seg_ps[:, 0:P]))
                dve.sem_inc(gadj_used)
                with dve.Fori(0, T) as t:
                    dve.wait_ge(gadj_in, t * 16 + 16)
                    link = Chain(dve, c_gen)
                    link.then(dve.tensor_scalar(e_wide, t_all, tile(EN, t, slice(D + 1, D + 2)), None, ALU.add))
                    link.then(dve.scalar_tensor_tensor(e_wide, e_wide, NEG_SLOPE, e_wide, ALU.mult, ALU.max))
                    link.then(dve.scalar_tensor_tensor(e_wide, row_in[:, 0, :], 0.0, e_wide, ALU.is_gt, ALU.mult))
                    link.then(dve.tensor_scalar(wide, row_in[:, 0, :], 0.0, 1.0, ALU.is_gt, ALU.subtract))
                    link.then(dve.scalar_tensor_tensor(e_wide, wide, -MASKED, e_wide, ALU.mult, ALU.add))
                    dve.sem_inc(gadj_used)
                    link.then(dve.tensor_reduce(zmax[:, :], e_wide, AX, ALU.max))
                    link.then(dve.tensor_scalar(neg_max[:, 0:1], zmax[:, :], -1.0, None, ALU.mult))
                    dve.sem_inc(gmax1_made)
                    dve.wait_ge(gprob_made, t + 1)
                    settled(dve, "dve")
                    with dve.Fori(0, T) as j:
                        link = Chain(dve, c_gen)
                        link.then(dve.tensor_copy(h1, e_wide[:, bass.ds(j * P, P)]))
                        dve.sem_inc(gprob_ready)
                        dve.wait_ge(gprobT_ps, t * T + j + 1)
                        link.then(dve.tensor_copy(h1T, emb_ps[:, 0:P]))
                        dve.sem_inc(gprobT_saved)
                    dve.wait_ge(gnum_made, t + 1)
                    link = Chain(dve, c_gen)
                    link.then(dve.reciprocal(dn[:, 1:2], den[:, 0:1]))
                    link.then(dve.tensor_scalar(num[:, 1, :], seg_ps[:, 0:D], dn[:, 1:2], 0.0, ALU.mult, ALU.max))
                    dve.wait_ge(gout_stored, t * 16 + 16)
                    link.then(dve.tensor_tensor(O[:, 0, :], num[:, 1, :], tile(X, t), ALU.add))
                    dve.sem_inc(gout_made)

        @block.tensor
        def _(pe):
            pe.wait_ge(cst_made, 1)
            pe.wait_ge(w_in, 48)
            pe.transpose(emb_ps[:, 0:D], Wsb[:, :], ident)
            pe.matmul(emb_ps[:, D:D + 1], Wsb[:, :], asb[:, 1:2], start=True, stop=True)
            pe.matmul(emb_ps[:, D + 1:D + 2], Wsb[:, :], asb[:, 0:1], start=True, stop=True).then_inc(wx_ps_made, 1)

            def codes(i, q, u):
                pe.wait_ge(diag_cleared, i * 2 + u + 1)
                if u == 0:
                    wait(pe, keys_taken, i)
                keys = key_ps[:, u * GROUPS:(u + 1) * GROUPS]
                pe.matmul(keys, ones_b[:, :], key_row[:, :], start=True, stop=False)
                for k in range(BITS):
                    ins = pe.matmul(keys, code_w[:, k, :], mask[:, q, u, k * GROUPS:(k + 1) * GROUPS], start=False, stop=(k == BITS - 1))
                ins.then_inc(keys_made, 1)
            codes(0, 0, 0)
            codes(0, 0, 1)

            def turn_gathered(i, q, u):
                wait(pe, scanned, i * 2 + u)
                for b in range(BLOCKS):
                    pe.wait_ge(gathered[q][u * BLOCKS + b], (i - q) * 8 + 16)
                    ins = pe.transpose(gt_ps[:, b * P:(b + 1) * P], G[:, q, u, b, 0:D], ident)
                ins.then_inc(gt_made, 1)

            def turn_back(i, u):
                pe.wait_ge(scanned, i * 2 + u + 1)
                for b in range(BLOCKS):
                    ins = pe.transpose(back_ps[:, b * P:(b + 1) * P], scan[:, b * P:(b + 1) * P], ident)
                ins.then_inc(back_made, 1)

            def pick_ends(i, u):
                pe.wait_ge(back_saved, i * 2 + u + 1)
                pe.wait_ge(ends_made, i * 2 + u + 1)
                if u == 0:
                    wait(pe, seg_taken, i)
                for b in range(BLOCKS):
                    ins = pe.matmul(seg_ps[:, u * D:(u + 1) * D], S[:, u, b, :], scanT[:, u, b, :], start=(b == 0), stop=(b == BLOCKS - 1))
                ins.then_inc(seg_made, 1)

            def cuts(i, u):
                for lo, hi in ((0, 512), (512, EDGES)):
                    pe.matmul(back_ps[:, lo:hi], cut_w[:, 0, :], ge_s[:, u, lo + 2:hi + 2], start=True, stop=False)
                    ins = pe.matmul(back_ps[:, lo:hi], cut_w[:, 1, :], ge_s[:, u, lo + 1:hi + 1], start=False, stop=True)
                ins.then_inc(cut_made, 1)

            def step(i, q):
                if within(i, -3):
                    e = i - 3
                    pe.wait_ge(h1_made, e + 1)
                    if isinstance(e, int) and e == 0:
                        pe.wait_ge(wx_saved, 1)
                    wait(pe, emb_saved, e)
                    for u in range(2):
                        ins = pe.transpose(emb_ps[:, u * P:(u + 1) * P], h1p[:, u, :], ident)
                    ins.then_inc(h1T_made, 1)
                if within(i, -2):
                    p = i - 2
                    turn_gathered(p, q, 0)
                if within(i, -3):
                    pe.wait_ge(h1T_saved, e + 1)
                    for u in range(2):
                        ins = pe.matmul(emb_ps[:, u * (D + 2):(u + 1) * (D + 2)], h1Tp[:, u, :], WX[:, :], start=True, stop=True)
                    ins.then_inc(emb_made, 1)
                if within(i, 1):
                    codes(i + 1, 1 - q, 0)
                if within(i, -2):
                    if not isinstance(i, int):
                        pe.wait_ge(cut_saved, i * 2)
                    else:
                        wait(pe, cut_saved, min(i, PAIRS) * 2)
                    turn_back(p, 0)
                    turn_gathered(p, q, 1)
                if within(i, 1):
                    codes(i + 1, 1 - q, 1)
                if within(i, -2):
                    pe.wait_ge(back_saved, p * 2 + 1)
                    turn_back(p, 1)
                    pick_ends(p, 0)
                if within(i, 0):
                    pe.wait_ge(counted, i + 1)
                    wait(pe, lists_taken, i)
                    pe.matmul(list_ps[:, 0:2], tri[:, :], V[:, :, 18], start=True, stop=True).then_inc(start_made, 1)
                if within(i, -2):
                    pick_ends(p, 1)
                if within(i, 0):
                    pe.wait_ge(spans_made, i + 1)
                    for u in range(2):
                        for b in range(BLOCKS):
                            at = 8 + 20 * (u * BLOCKS + b)
                            edges = slice(2 + b * P, 2 + (b + 1) * P)
                            pe.matmul(list_ps[:, at:at + 19], ge_s[:, u, edges], V[:, u, 0:19], start=True, stop=False)
                            ins = pe.matmul(list_ps[:, at:at + 19], ge_e[:, u, edges], NV[:, u, 0:19], start=False, stop=True)
                    ins.then_inc(lists_made, 1)
                    if not within(i, -2):
                        wait(pe, cut_saved, i * 2)
                    cuts(i, 0)
                    pe.wait_ge(cut_saved, i * 2 + 1)
                    cuts(i, 1)
            steps(pe, step, PAIRS + 3, 4, 1)

            pe.wait_ge(checked, 1)
            pe.matmul(list_ps[:, 0:1], ones[:, :], bad_row[:, :], start=True, stop=True).then_inc(bad_summed, 1)

            def targets(t, q, u):
                wait(pe, z_made, t - 1)
                for b in range(BLOCKS):
                    pe.wait_ge(gathered[q][u * BLOCKS + b], (t - u - 2 * q) * 4 + 16 * (PAIRS // 2) + 16)
                    ins = pe.matmul(tb_ps[u][:, b * P:(b + 1) * P], G[:, q, u, b, D:D + 1].broadcast_to([P, P]), ident, start=True, stop=True)
                ins.then_inc(tb_made, 1)

            def product(t, q, u):
                pe.wait_ge(probs_made, t + 1)
                wait(pe, probT_saved, t)
                for b in range(BLOCKS):
                    ins = pe.transpose(gt_ps[:, b * P:(b + 1) * P], prob[:, u, b * P:(b + 1) * P], ident)
                ins.then_inc(probT_made, 1)
                pe.wait_ge(probT_saved, t + 1)
                wait(pe, num_taken, t)
                for b in range(BLOCKS):
                    ins = pe.matmul(seg_ps[:, 0:D], probT[:, u, b, :], G[:, q, u, b, 0:D], start=(b == 0), stop=(b == BLOCKS - 1))
                ins.then_inc(num_made, 1)

            targets(0, 0, 0)

            def step1(i, q):
                if within(i, -1):
                    product(i * 2 - 1, 1 - q, 1)
                targets(i * 2 + 1, q, 1)
                product(i * 2, q, 0)
                if within(i, 1):
                    targets(i * 2 + 2, 1 - q, 0)
            steps(pe, step1, PAIRS, 2, 2)
            product(T - 1, 1, 1)

            with pe.If(flag(pe) > 0):
                with pe.Fori(0, T) as t:
                    pe.wait_ge(gh_ready, t + 1)
                    pe.transpose(emb_ps[:, 0:P], h1, ident).then_inc(ghT_ps, 1)
                with pe.Fori(0, T) as t:
                    pe.wait_ge(gmax_made, t + 1)
                    pe.transpose(seg_ps[:, 0:D], aggT, ident).then_inc(gagg_made, 1)
                with pe.Fori(0, T) as t:
                    pe.wait_ge(gh1_made, t + 1)
                    pe.transpose(emb_ps[:, 0:P], h1, ident).then_inc(gh1T_ps, 1)
                    pe.wait_ge(gh1T_saved, t + 1)
                    pe.matmul(emb_ps[:, P:P + D + 2], h1T, WX[:, :], start=True, stop=True).then_inc(gemb_ps, 1)
                    pe.wait_ge(gt_ready, t + 1)
                    pe.matmul(seg_ps[:, 0:P], zmax[:, 0:1].broadcast_to([P, P]), ident, start=True, stop=True).then_inc(gt_ps_made, 1)
                with pe.Fori(0, T) as t:
                    def product(j, first, last):
                        pe.wait_ge(gprob_ready, t * T + j + 1)
                        pe.transpose(emb_ps[:, 0:P], h1, ident).then_inc(gprobT_ps, 1)
                        pe.wait_ge(gprobT_saved, t * T + j + 1)
                        ins = pe.matmul(seg_ps[:, 0:D], h1T, tile(EN, j, slice(0, D)), start=first, stop=last)
                        if last:
                            ins.then_inc(gnum_made, 1)
                    product(0, True, False)
                    with pe.Fori(0, T - 2) as j:
                        product(j + 1, False, False)
                    product(T - 1, False, True)


def kernel(**inputs):
    import numpy as _np
    import concourse.bacc as _bacc
    from concourse import mybir as _mybir
    from concourse.bass_utils import run_bass_kernel_spmd as _run

    nc = _bacc.Bacc("TRN2", target_bir_lowering=False, num_devices=1)
    arrays, args = {}, []
    given = {n: inputs[n] for n in ("x", "adj", "L1_gnn_W", "L1_gnn_a")}
    given["constants"] = constants()
    for name, value in given.items():
        a = _np.ascontiguousarray(value)
        arrays[f"in_{name}_dram"] = a
        args.append(nc.dram_tensor(f"in_{name}_dram", a.shape, _mybir.dt.from_np(a.dtype), kind="ExternalInput").ap())
    args.append(nc.dram_tensor("out_0_dram", (N, D), _mybir.dt.float32, kind="ExternalOutput").ap())
    args.append(nc.dram_tensor("h_rows", (N, D), _mybir.dt.float32, kind="Internal").ap())
    args.append(nc.dram_tensor("e_rows", (N, ROWLEN), _mybir.dt.float32, kind="Internal").ap())
    build(nc, *args)
    r = _run(nc, [arrays], core_ids=[0])
    return r.results[0]["out_0_dram"]
```

```python
import concourse.bass as bass
from concourse import mybir
from contextlib import ExitStack

F32, I32 = mybir.dt.float32, mybir.dt.int32
BF16, F16 = mybir.dt.bfloat16, mybir.dt.float16
ALU = mybir.AluOpType
ACT = mybir.ActivationFunctionType
AX = mybir.AxisListType.X

P = 128
N = 4096
T = N // P
D = 128
HALF = N // 2
GROUPS = 256
BITS = N // GROUPS
LEVELS = 3
SLOTS = 16
BLOCKS = 5
EDGES = BLOCKS * P
SHARE = BLOCKS - 1
PBLOCKS = 2 * BLOCKS - 1
E2 = EDGES + 2
ROWLEN = D + 2
EW = D + 1
NEG_SLOPE = 0.01
EPS = 1e-5
HMAX = 64.0
BIG = 1e30
MASKED = -9e16
PAIRS = T // 2
OFF = 0.375
BASE = OFF * OFF

LEAD = 6
EARLY = 2

C_ID, C_TRI, C_ROW1, C_IOTA, C_G = 0, P, 2 * P, 3 * P, 3 * P + EDGES
C_PB = C_G + GROUPS
C_S = C_PB + BLOCKS
C_P1 = C_S + SLOTS
CONSTS = C_P1 + 1


def constants():
    import numpy as np
    c = np.zeros((P, CONSTS), np.float32)
    p = np.arange(P, dtype=np.float32)[:, None]
    c[:, C_ID:C_ID + P] = np.eye(P)
    c[:, C_TRI:C_TRI + P] = np.triu(np.ones((P, P)), 1)
    c[:, C_ROW1:C_ROW1 + P] = np.arange(P)[None] + 1
    c[:, C_IOTA:C_IOTA + EDGES] = np.arange(EDGES)[None]
    c[0, C_G:C_G + GROUPS] = np.arange(GROUPS)
    c[1, C_G:C_G + GROUPS] = -BASE * 2 ** (BITS + 10)
    c[2, C_G:C_G + GROUPS] = BASE * 2 ** 10
    c[:, C_PB:C_PB + BLOCKS] = p + P * np.arange(BLOCKS)[None]
    c[:, C_S:C_S + SLOTS] = np.arange(SLOTS)[None]
    c[:, C_P1:C_P1 + 1] = p + 1
    return c


class Chain:

    def __init__(self, eng, sem):
        self.eng, self.sem, self.n, self.seen = eng, sem, 0, 0
        eng.sem_inc(sem)
        eng.sem_clear(sem)

    def did(self, ins):
        ins.then_inc(self.sem, 1)
        self.n += 1
        return self.n

    def need(self, n):
        if self.seen < n:
            self.eng.wait_ge(self.sem, n)
            self.seen = n

    def then(self, ins):
        self.need(self.did(ins))

    def wait(self):
        self.need(self.n)


def build(nc, x, adj, W, a, consts, out, h_rows, e_rows):
    ctx = ExitStack()
    with ctx:
        def sb(name, shape, dt=F32):
            return ctx.enter_context(nc.sbuf_tensor(name, shape, dt))

        def ps(name, cols):
            return ctx.enter_context(nc.psum_tensor(name, [P, cols], F32))

        def sem(name):
            return ctx.enter_context(nc.semaphore(name))

        cst = sb("cst", [P, CONSTS])
        ident = cst[:, C_ID:C_ID + P]
        row1 = cst[:, C_ROW1:C_ROW1 + P]
        edge_pb = cst[:, C_PB:C_PB + BLOCKS]
        slot_iota = cst[:, C_S:C_S + SLOTS]
        code_w = sb("code_w", [P, BITS, P], BF16)
        key_row = sb("key_row", [P, GROUPS], BF16)
        ones_b = sb("ones_b", [P, P], BF16)
        diag_cap = sb("diag_cap", [P, P], BF16)
        tri = sb("tri", [P, P], F16)
        iota_e = sb("iota_e", [P, EDGES], F16)
        cut_w = sb("cut_w", [P, 2, P], F16)
        adj_in = sb("adj_in", [P, 2, N], I32)
        mask = sb("mask", [P, 2, 2, N], BF16)
        X = sb("X", [P, T, D])
        H = sb("H", [P, T, D])
        EN = sb("EN", [P, T, D + 2])
        G = sb("G", [P, 2, PBLOCKS, EW])
        stat6 = sb("stat6", [P, 4, 6])
        mv = sb("mv", [P, T, 2])
        mv1 = sb("mv1", [P, 2, 2])
        std = sb("std", [P, T])
        rstd = sb("rstd", [P, T])
        eps = sb("eps", [P, 1])
        minus_off = sb("minus_off", [P, 1])
        nmr = sb("nmr", [P, T])
        deg = sb("deg", [P, T, 2])
        cnt = sb("cnt", [P, T])
        start = sb("start", [P, T])
        end = sb("end", [P, T])
        carry = sb("carry", [P, 1])
        rest = sb("rest", [P, T])
        last_row = sb("last_row", [P, T, BLOCKS])
        idx_all = sb("idx_all", [P, T, BLOCKS], I32)
        idx = [sb(f"idx{q}", [P, 2 * BLOCKS], I32) for q in range(2)]
        top = sb("top", [P, 2, SLOTS])
        keys2 = sb("keys2", [P, 2, GROUPS])
        topi = sb("topi", [P, 2, SLOTS], I32)
        grp = sb("grp", [P, 2, SLOTS], I32)
        powr = sb("powr", [P, LEVELS, 2 * SLOTS], I32)
        rem = sb("rem", [P, LEVELS, 2 * SLOTS])
        shf = sb("shf", [P, LEVELS, 2 * SLOTS], I32)
        cand = sb("cand", [P, 2, LEVELS, SLOTS])
        cand2 = sb("cand2", [P, 2, LEVELS * SLOTS])
        val = sb("val", [P, 2, SLOTS])
        valid = sb("valid", [P, 2, SLOTS])
        V = sb("V", [P, 2, 20], F16)
        NV = sb("NV", [P, 2, 20], F16)
        ge_s = sb("ge_s", [P, 2, E2], F16)
        ge_e = sb("ge_e", [P, 2, E2], F16)
        kpos = sb("kpos", [P, 2 * BLOCKS])
        onehot = sb("onehot", [P, 2 * BLOCKS, SLOTS])
        pick = sb("pick", [P, 2 * BLOCKS, SLOTS])
        red = sb("red", [P, 2 * BLOCKS])
        lastm = sb("lastm", [P, 2 * BLOCKS])
        cut = sb("cut", [P, 2, 2, EDGES], BF16)
        scan = sb("scan", [P, EDGES])
        scanT = sb("scanT", [P, 2, BLOCKS, P])
        S = sb("S", [P, 2, 2, BLOCKS, P])
        agg = sb("agg", [P, 2, D])
        h1p = sb("h1p", [P, 2, D])
        h1Tp = sb("h1Tp", [P, 2, P])
        h1, h1T = h1p[:, 0, :], h1Tp[:, 0, :]
        WX = sb("WX", [P, D + 2])
        Wsb = sb("Wsb", [P, D])
        asb = sb("asb", [P, 2])
        work = adj_in[:, :, :].rearrange("p q n -> p (q n)").bitcast(F32)
        work = work[:, 0:10 * EDGES].rearrange("p (k q e) -> p k q e", k=5, q=2)
        z, exp_pos, exp_neg, prob = (work[:, k] for k in range(4))
        probT = work[:, 4].rearrange("p q (b d) -> p q b d", b=BLOCKS)
        off_s, off_e, off = (sb(n, [P, EDGES], BF16) for n in ("off_s", "off_e", "off"))
        zmax = sb("zmax", [P, 1])
        lin = sb("lin", [P, 2])
        neg_max = sb("neg_max", [P, 2])
        bias = sb("bias", [P, 2, 2])
        src01 = sb("src01", [P, T])
        xself = sb("xself", [P, T])
        wself = sb("wself", [P, 2])
        den = sb("den", [P, 2])
        dn = sb("dn", [P, 2])
        num = sb("num", [P, 2, D])
        O = sb("O", [P, 2, D])
        junk = sb("junk", [P, 2 * T])

        bad = sb("bad", [P, 4, T])
        bad_row = sb("bad_row", [P, 1])
        general = sb("general", [P, 1], I32)
        ones = sb("ones", [P, P])
        ones_h = sb("ones_h", [P, P], F16)
        row_in = adj_in
        hT = EN[:, :, :].rearrange("p t d -> p (t d)")[:, 0:N]
        wide = mask[:, 0, :, :].rearrange("p u n -> p (u n)").bitcast(F32)
        e_wide = adj_in[:, 1, :].bitcast(F32)
        t_all = H[:, :, :].rearrange("p t d -> p (t d)")
        aggT = h1T

        front_ps = ps("front_ps", 1024)
        key_ps = front_ps[:, 0:512]
        emb_ps = front_ps[:, 512:1024]
        list_ps = ps("list_ps", 512)
        gt_ps = ps("gt_ps", 1024)
        back_ps = ps("back_ps", 1024)
        seg_ps = ps("seg_ps", 512)
        LB = list_ps[:, 8:8 + 40 * BLOCKS].rearrange("p (b v) -> p b v", v=20)
        tb_ps = [back_ps, front_ps]
        seg2 = seg_ps[:, 0:2 * D].rearrange("p (u d) -> p u d", u=2)

        cst_in, x_in, w_in = sem("cst_in"), [sem(f"x_in{c}") for c in range(4)], sem("w_in")
        cst_made = sem("cst_made")
        adj_loaded = [[sem(f"adj_loaded{q}{h}") for h in range(2)] for q in range(2)]
        signed = sem("signed")
        diag_cleared = sem("diag_cleared")
        keys_made, keys_taken = sem("keys_made"), sem("keys_taken")
        counted, start_made, spans_made = sem("counted"), sem("start_made"), sem("spans_made")
        lists_made, lists_taken = sem("lists_made"), sem("lists_taken")
        idx_ready = sem("idx_ready")
        cut_made, cut_saved = sem("cut_made"), sem("cut_saved")
        gathered = [[sem(f"gathered{q}_{b}") for b in range(PBLOCKS)] for q in range(2)]
        gt_made, scanned = sem("gt_made"), sem("scanned")
        back_made, back_saved = sem("back_made"), sem("back_saved")
        ends_made, seg_made, seg_taken = sem("ends_made"), sem("seg_made"), sem("seg_taken")
        x1_stats, std1_made, rstd1_made, h1_made, h1T_made, h1T_saved = (sem("x1_stats"), sem("std1_made"), sem("rstd1_made"), sem("h1_made"), sem("h1T_made"), sem("h1T_saved"))
        emb_made, emb_saved, emb_stored = sem("emb_made"), sem("emb_saved"), [sem("emb_stored0"), sem("emb_stored1")]
        std0_made = sem("std0_made")
        stats0, h0_made, h0_made2, h0_stored = sem("stats0"), sem("h0_made"), sem("h0_made2"), sem("h0_stored")
        wx_ps_made, wx_saved = sem("wx_ps_made"), sem("wx_saved")
        c_ln, c_set, c_keys, c_span, c_list, c_seg = (sem(n) for n in ("c_ln", "c_set", "c_keys", "c_span", "c_list", "c_seg"))
        idx2_ready, tb_made, z_made, m_made = sem("idx2_ready"), sem("tb_made"), sem("z_made"), sem("m_made")
        c_z = sem("c_z")
        probT_made, probT_saved, num_made, num_taken = (sem(n) for n in ("probT_made", "probT_saved", "num_made", "num_taken"))
        scales0, idx_kept, probs_made = sem("scales0"), sem("idx_kept"), sem("probs_made")
        self_made, exps_made = sem("self_made"), sem("exps_made")
        out_made, out_stored = sem("out_made"), [sem("out_stored0"), sem("out_stored1")]

        passed = {"pool": sem("pool_passed"), "dve": sem("dve_passed")}

        def settled(eng, who):
            eng.sem_inc(passed[who])

        checked, bad_summed, flag_made = sem("checked"), sem("bad_summed"), sem("flag_made")
        gx_in, gh_ready, ghT_ps = sem("gx_in"), sem("gh_ready"), sem("ghT_ps")
        grow_in = [sem("grow_in0"), sem("grow_in1")]
        grow_used, gmax_made, gagg_made = sem("grow_used"), sem("gmax_made"), sem("gagg_made")
        c_gen = sem("c_gen")
        gvar_made, gstd_made, gh1_made, gh1T_ps, gh1T_saved = (sem(n) for n in ("gvar_made", "gstd_made", "gh1_made", "gh1T_ps", "gh1T_saved"))
        gemb_ps, gt_ps_made = sem("gemb_ps"), sem("gt_ps_made")
        gadj_in, gadj_used, gmax1_made, gprob_made = (sem(n) for n in ("gadj_in", "gadj_used", "gmax1_made", "gprob_made"))
        gt_ready, gprob_ready = sem("gt_ready"), sem("gprob_ready")
        gprobT_ps, gprobT_saved, gnum_made, gout_made, gout_stored = (sem(n) for n in ("gprobT_ps", "gprobT_saved", "gnum_made", "gout_made", "gout_stored"))

        block = ctx.enter_context(nc.Block())

        x_v = x.rearrange("(t p) d -> p t d", p=P)
        out_v = out.rearrange("(t p) d -> p t d", p=P)
        h_v = h_rows.rearrange("(t p) d -> p t d", p=P)
        e_v = e_rows.rearrange("(t p) d -> p t d", p=P)
        adj_v = adj.rearrange("(t p) n -> p t n", p=P)

        def wait(eng, s, value):
            if isinstance(value, int) and value <= 0:
                return
            eng.wait_ge(s, value)

        def steps(eng, step, last, lead, ahead):
            hi = PAIRS - ahead
            hi -= (hi - lead) % 2
            for i in range(lead):
                step(i, i % 2)
            with eng.Fori(0, (hi - lead) // 2) as turn:
                for u in range(2):
                    step(turn * 2 + (lead + u), (lead + u) % 2)
            for i in range(hi, last):
                step(i, i % 2)

        def within(i, off):
            return not isinstance(i, int) or 0 <= i + off < PAIRS

        def early(i):
            return isinstance(i, int) and i < EARLY

        def pair(buf, i, cols=slice(None)):
            return buf[:, bass.ds(i * 2, 2), cols] if len(buf.shape) == 3 else buf[:, bass.ds(i * 2, 2)]

        XC = 4
        TC = T // XC

        def flag(eng):
            eng.wait_ge(flag_made, 1)
            return eng.value_load(general[0:1, 0:1], min_val=0, max_val=1 << 20)

        def tile(buf, t, cols=slice(None)):
            return buf[:, bass.ds(t, 1), cols].rearrange("p a d -> p (a d)")

        @block.sync
        def _(sp):
            for c in range(XC):
                sp.dma_start(X[:, c * TC:(c + 1) * TC, :], x_v[:, c * TC:(c + 1) * TC, :]).then_inc(x_in[c], 16)
                if c == 0:
                    sp.dma_start(cst[:, :], consts).then_inc(cst_in, 16)
            sp.dma_start(Wsb[:, :], W).then_inc(w_in, 16)
            for h in range(2):
                sp.dma_start(asb[:, h:h + 1], a[h * P:(h + 1) * P, :]).then_inc(w_in, 16)

            def load_half(i, u, h):
                t = i * 2 + u
                wait(sp, signed, (t - 2) * 2 + h + 1)
                sp.dma_start(adj_in[:, u, h * HALF:(h + 1) * HALF],
                             tile(adj_v, t, slice(h * HALF, (h + 1) * HALF))).then_inc(adj_loaded[u][h], 16)

            def load(i):
                for u in range(2):
                    for h in range(2):
                        load_half(i, u, h)

            load(0)
            for c in range(XC):
                if c < XC // 2:
                    sp.wait_ge(h0_made, c + 1)
                else:
                    sp.wait_ge(h0_made2, c + 1 - XC // 2)
                sp.dma_start(h_v[:, c * TC:(c + 1) * TC, :], H[:, c * TC:(c + 1) * TC, :]).then_inc(h0_stored, 16)
                load_half(1, c // 2, c % 2)

            def step(i, q):
                if within(i, 2):
                    load(i + 2)
                if within(i, -5):
                    sp.wait_ge(emb_saved, i - 4)
                    sp.dma_start(pair(e_v, i - 5), pair(EN, i - 5)).then_inc(emb_stored[q], 16)
            steps(sp, step, PAIRS + 5, LEAD, 2)

            with sp.Fori(0, PAIRS) as i:
                for u in range(2):
                    sp.wait_ge(out_made, i * 2 + u + 1)
                    sp.dma_start(tile(out_v, i * 2 + u), O[:, u, :]).then_inc(out_stored[u], 16)
            for q in range(2):
                sp.wait_ge(out_stored[q], 16 * T // 2)

            with sp.If(flag(sp) > 0):
                sp.dma_start(X[:, :, :], x_v).then_inc(gx_in, 16)
                with sp.Fori(0, N // 2) as duo:
                    sp.wait_ge(grow_used, duo * 2 + 1)
                    for u in range(2):
                        sp.dma_start(row_in[:, u, :], adj[bass.ds(duo * 2 + u, 1), :].broadcast_to([P, N])).then_inc(grow_in[u], 16)
                with sp.Fori(0, T) as t:
                    sp.wait_ge(gadj_used, t + 1)
                    sp.dma_start(row_in[:, 0, :], tile(adj_v, t)).then_inc(gadj_in, 16)
                    sp.wait_ge(gout_made, t + 1)
                    sp.dma_start(tile(out_v, t), O[:, 0, :]).then_inc(gout_stored, 16)
                sp.wait_ge(gout_stored, 16 * T + 16)

        @block.gpsimd
        def _(pool):
            pool.wait_ge(h0_stored, 16 * XC)

            def gather(table, width, q, blocks):
                for b in blocks:
                    k = b if b <= SHARE else b + 1
                    pool.indirect_dma_start(out=G[:, q, b, 0:width], out_offset=None, in_=table,
                                            in_offset=bass.IndirectOffsetOnAxis(ap=idx[q][:, k:k + 1], axis=0)).then_inc(gathered[q][b], 16)

            def step(i, q):
                pool.wait_ge(idx_ready, i + 1)
                for u, blocks in enumerate((range(SHARE), range(SHARE, PBLOCKS))):
                    wait(pool, gt_made, i * 2 + u - 3)
                    settled(pool, "pool")
                    gather(h_rows, D, q, blocks)
            steps(pool, step, PAIRS, 2, 0)
            for q in range(2):
                pool.wait_ge(emb_stored[q], 16 * PAIRS // 2)

            def step1(i, q):
                pool.wait_ge(idx2_ready, i + 1)
                for u, blocks in enumerate((range(SHARE), range(SHARE, PBLOCKS))):
                    wait(pool, num_made, i * 2 + u - 3)
                    settled(pool, "pool")
                    gather(e_rows, EW, q, blocks)
            steps(pool, step1, PAIRS, 2, 0)

        @block.scalar
        def _(act):
            def square(i, q, u, h):
                t = i * 2 + u
                act.wait_ge(adj_loaded[u][h], i * 16 + 16)
                wait(act, keys_made, t - 3)
                act.activation(mask[:, q, u, h * HALF:(h + 1) * HALF], adj_in[:, u, h * HALF:(h + 1) * HALF], ACT.Square,
                               bias=minus_off[:, :], accum_out=tile(deg, t, slice(h, h + 1))).then_inc(signed, 1)

            def inverse(c):
                ts = slice(c * TC, (c + 1) * TC)
                act.wait_ge(stats0, c + 1)
                act.activation(std[:, ts], mv[:, ts, 1], ACT.Sqrt, bias=eps[:, :]).then_inc(std0_made, 1)

            for c in range(XC // 2):
                inverse(c)
                act.wait_ge(scales0, c + 1)
                for t in range(c * TC, (c + 1) * TC):
                    ins = act.activation(H[:, t, :], X[:, t, :], ACT.Relu, bias=nmr[:, t:t + 1], scale=rstd[:, t:t + 1])
                ins.then_inc(h0_made, 1)
            for c in range(XC // 2, XC):
                inverse(c)
            for u in range(2):
                for h in range(2):
                    square(0, 0, u, h)
            act.wait_ge(wx_ps_made, 1)
            act.activation(WX[:, :], emb_ps[:, 0:D + 2], ACT.Copy).then_inc(wx_saved, 1)
            for u in range(2):
                for h in range(2):
                    square(1, 1, u, h)

            def save_scan(i, u):
                act.wait_ge(back_made, i * 2 + u + 1)
                wait(act, seg_made, i * 2 + u - 1)
                act.activation(scanT[:, u, :, :].rearrange("p b d -> p (b d)"), back_ps[:, 0:EDGES], ACT.Copy).then_inc(back_saved, 1)

            def save_cut(i, q, u):
                act.wait_ge(cut_made, i * 2 + u + 1)
                wait(act, scanned, i * 2 + u - 3)
                act.activation(cut[:, q, u, :], back_ps[:, 0:EDGES], ACT.Copy).then_inc(cut_saved, 1)

            def step(i, q):
                def squares(halves, when):
                    if when and within(i, 2):
                        for u, h in halves:
                            square(i + 2, q, u, h)

                late = early(i)
                squares(((0, 0), (0, 1)), not late)
                if within(i, -2):
                    save_scan(i - 2, 0)
                if within(i, -4):
                    e = i - 4
                    act.wait_ge(h1T_made, e + 1)
                    act.activation(h1Tp[:, :, :].rearrange("p u d -> p (u d)"), emb_ps[:, 0:2 * P], ACT.Copy).then_inc(h1T_saved, 1)
                squares(((1, 0),), not late)
                if within(i, -2):
                    save_scan(i - 2, 1)
                squares(((1, 1),), not late)
                if within(i, -3):
                    r = i - 3
                    act.wait_ge(x1_stats, r + 1)
                    act.activation(pair(std, r), mv1[:, :, 1], ACT.Sqrt, bias=eps[:, :]).then_inc(std1_made, 1)
                    wait(act, h1T_made, r)
                    for u in range(2):
                        ins = act.activation(h1p[:, u, :], tile(X, r * 2 + u), ACT.Relu, bias=nmr[:, bass.ds(r * 2 + u, 1)])
                    ins.then_inc(h1_made, 1)
                squares(((0, 0), (0, 1)), late)
                if within(i, 0):
                    save_cut(i, q, 0)
                if within(i, -4):
                    act.wait_ge(emb_made, e + 1)
                    act.wait_ge(rstd1_made, e + 1)
                    for u in range(2):
                        ins = act.activation(tile(EN, e * 2 + u), emb_ps[:, u * (D + 2):(u + 1) * (D + 2)], ACT.Copy,
                                             scale=rstd[:, bass.ds(e * 2 + u, 1)])
                    ins.then_inc(emb_saved, 1)
                if within(i, 0):
                    save_cut(i, q, 1)
                squares(((1, 0), (1, 1)), late)
            steps(act, step, PAIRS + 4, LEAD, 2)

            def tile1(t, u):
                if not isinstance(t, int) or t >= 1:
                    act.wait_ge(probT_made, t)
                    wait(act, num_made, t - 2)
                    act.activation(probT[:, 1 - u, :, :].rearrange("p b d -> p (b d)"), gt_ps[:, 0:EDGES], ACT.Copy).then_inc(probT_saved, 1)
                if not isinstance(t, int) or t < T:
                    act.wait_ge(m_made, t + 1)
                    wait(act, probs_made, t - 1)
                    act.activation(exp_pos[:, u, :], z[:, u, :], ACT.Exp, bias=bias[:, u, 0:1])
                    act.activation(exp_neg[:, u, :], z[:, u, :], ACT.Exp, bias=bias[:, u, 1:2], scale=NEG_SLOPE)
                    wait(act, out_made, t - 1)
                    act.activation(wself[:, u:u + 1], xself[:, bass.ds(t, 1)], ACT.Exp, bias=neg_max[:, u:u + 1]).then_inc(exps_made, 1)

            act.wait_ge(self_made, 1)

            def step1(i, q):
                for u in range(2):
                    tile1(i * 2 + u, u)
            steps(act, step1, PAIRS, 2, 0)
            tile1(T, 0)

            with act.If(flag(act) > 0):
                with act.Fori(0, T) as t:
                    act.wait_ge(gvar_made, t + 1)
                    act.activation(std[:, bass.ds(t, 1)], mv1[:, 0, 1:2], ACT.Sqrt, bias=eps[:, :]).then_inc(gstd_made, 1)
                    act.activation(h1, tile(X, t), ACT.Relu, bias=nmr[:, bass.ds(t, 1)]).then_inc(gh1_made, 1)
                    act.wait_ge(gh1T_ps, t + 1)
                    act.activation(h1T, emb_ps[:, 0:P], ACT.Copy).then_inc(gh1T_saved, 1)
                with act.Fori(0, T) as t:
                    act.wait_ge(gmax1_made, t + 1)
                    act.activation(e_wide, e_wide, ACT.Exp, bias=neg_max[:, 0:1], accum_out=den[:, 0:1]).then_inc(gprob_made, 1)

        @block.vector
        def _(dve):
            def means(link, t):
                at = t % 4
                done = [link.did(dve.bn_stats(stat6[:, at + u, :], X[:, t + u, :])) for u in range(2)]
                for u in range(2):
                    link.need(done[u])
                    link.did(dve.bn_aggr(mv[:, t + u, :], stat6[:, at + u, :]))

            def scales(c):
                ts = slice(c * TC, (c + 1) * TC)
                dve.wait_ge(std0_made, c + 1)
                link.then(dve.reciprocal(rstd[:, ts], std[:, ts]))
                link.did(dve.scalar_tensor_tensor(nmr[:, ts], mv[:, ts, 0], -1.0, rstd[:, ts], ALU.mult, ALU.mult))
                link.wait()
                dve.sem_inc(scales0)

            def relu_norm(c):
                for t in range(c * TC, (c + 1) * TC):
                    link.did(dve.tensor_scalar(H[:, t, :], X[:, t, :], rstd[:, t:t + 1], nmr[:, t:t + 1], ALU.mult, ALU.add))
                link.wait()
                piece = H[:, c * TC:(c + 1) * TC, :].rearrange("p t d -> p (t d)")
                dve.tensor_scalar(piece, piece, 0.0, None, ALU.max).then_inc(h0_made2, 1)

            dve.memset(minus_off[:, :], -OFF)
            dve.memset(eps[:, :], EPS)
            link = Chain(dve, c_ln)
            for c in range(XC):
                dve.wait_ge(x_in[c], 16)
                for t in range(c * TC, (c + 1) * TC, 2):
                    means(link, t)
                link.wait()
                dve.sem_inc(stats0)
                if c > 0:
                    scales(c - 1)

            dve.wait_ge(cst_in, 16)
            for k in range(BITS):
                dve.tensor_scalar(code_w[:, k, :], ident, float(2 ** (k + 10)), None, ALU.mult)
            dve.tensor_copy(key_row[:, :], cst[:, C_G:C_G + GROUPS])
            dve.tensor_scalar(diag_cap[:, :], ident, -4096.0, 4096.0 + BASE, ALU.mult, ALU.add)
            dve.memset(ones_b[:, :], 1.0).then_inc(cst_made, 1)
            dve.wait_ge(cst_made, 1)
            scales(XC - 1)

            def clear_diagonal(i, q, u):
                dve.wait_ge(signed, i * 4 + u * 2 + 2)
                blk = mask[:, q, u, bass.ds((i * 2 + u) * P, P)]
                dve.tensor_tensor(blk, blk, diag_cap[:, :], ALU.min).then_inc(diag_cleared, 1)

            def scan_max(i, q, u):
                dve.wait_ge(gt_made, i * 2 + u + 1)
                dve.wait_ge(cut_saved, i * 2 + u + 1)
                wait(dve, back_made, i * 2 + u)
                dve.tensor_tensor_scan(scan[:, :], cut[:, q, u, :], gt_ps[:, 0:EDGES], 0.0, ALU.add, ALU.max).then_inc(scanned, 1)

            def row_ends(i, q, u, part):
                lo, hi = ((0, 3), (3, BLOCKS))[part]
                last = last_row[:, bass.ds(i * 2 + u, 1), lo:hi].rearrange("p a b -> p b a").broadcast_to([P, hi - lo, P])
                dve.wait_ge(lists_taken, i + 1)
                dve.tensor_tensor(S[:, q, u, lo:hi, :], row1.rearrange("p (a r) -> p a r", a=1).broadcast_to([P, hi - lo, P]),
                                  last, ALU.is_equal).then_inc(ends_made, 1)

            def inverse_std(i):
                dve.wait_ge(std1_made, i + 1)
                dve.reciprocal(pair(rstd, i), pair(std, i)).then_inc(rstd1_made, 1)

            def residual(r):
                dve.wait_ge(seg_made, r * 2 + 2)
                dve.tensor_tensor(agg[:, :, :], seg2, pair(H, r), ALU.max).then_inc(seg_taken, 1)
                yield
                wait(dve, std1_made, r)
                dve.wait_ge(seg_taken, r + 1)
                link = Chain(dve, c_seg)
                link.did(dve.tensor_tensor(pair(X, r), pair(X, r), agg[:, :, :], ALU.add))
                yield
                link.wait()
                for u in range(2):
                    link.did(dve.bn_stats(stat6[:, u, :], tile(X, r * 2 + u)))
                    yield
                for u in range(2):
                    link.need(2 + u)
                    link.did(dve.bn_aggr(mv1[:, u, :], stat6[:, u, :]))
                    yield
                link.wait()
                dve.tensor_scalar(pair(nmr, r), mv1[:, :, 0], -1.0, None, ALU.mult).then_inc(x1_stats, 1)
                yield

            def read_keys(i, q):
                fill = within(i, -2)
                take = within(i, 0)
                more = residual(i - 3) if within(i, -3) else iter(())
                go = lambda: next(more, None)
                if take:
                    dve.wait_ge(keys_made, i * 2 + 2)
                    link = Chain(dve, c_keys)
                    keys = [key_ps[:, u * GROUPS:(u + 1) * GROUPS] for u in range(2)]
                    m = [link.did(dve.max(top[:, u, 0:8], keys[u])) for u in range(2)]
                    for u in range(2):
                        link.need(m[u])
                        m[u] = link.did(dve.match_replace(keys2[:, u, :], top[:, u, 0:8], keys[u], -1.0))
                    link.need(m[0])
                    link.did(dve.max(top[:, 0, 8:16], keys2[:, 0, :]))
                    link.need(m[1])
                    dve.sem_inc(keys_taken)
                    m = link.did(dve.max(top[:, 1, 8:16], keys2[:, 1, :]))
                if isinstance(i, int) and i == EARLY:
                    for u in range(2):
                        clear_diagonal(i + 1, 1 - q, u)
                if fill:
                    scan_max(i - 2, q, 0)
                left = top[:, :, :].rearrange("p u s -> p (u s)")
                for v in range(LEVELS):
                    if take:
                        link.need(m)
                        m = link.did(dve.tensor_scalar(powr[:, v, :], left.bitcast(I32), 0x7F800000, None, ALU.bitwise_and))
                    go()
                    if take:
                        link.need(m)
                        m = link.did(dve.tensor_tensor(rem[:, v, :], left, powr[:, v, :].bitcast(F32), ALU.subtract))
                        left = rem[:, v, :]
                        if v == 0:
                            k = link.did(dve.tensor_copy(topi[:, :, :], top[:, :, :]))
                        if v == 1:
                            link.need(k)
                            link.did(dve.tensor_scalar(grp[:, :, :], topi[:, :, :], GROUPS - 1, None, ALU.bitwise_and))
                if take:
                    k = link.did(dve.tensor_scalar(shf[:, :, :], powr[:, :, :], 15, None, ALU.logical_shift_right))
                go()
                if take:
                    link.need(m)
                    link.did(dve.tensor_reduce(pair(rest, i), rem[:, LEVELS - 1, :].rearrange("p (u s) -> p u s", u=2), AX, ALU.max))
                    link.need(k)
                    m = []
                    for u in range(2):
                        m.append(link.did(dve.scalar_tensor_tensor(
                            cand[:, u, :, :], shf[:, :, u * SLOTS:(u + 1) * SLOTS], float(1 - (127 + 8) * GROUPS),
                            grp[:, u:u + 1, :].broadcast_to([P, LEVELS, SLOTS]), ALU.add, ALU.add)))
                    cands = [cand[:, u, :, :].rearrange("p v s -> p (v s)") for u in range(2)]
                    for u in range(2):
                        link.need(m[u])
                        m[u] = link.did(dve.max(val[:, u, 0:8], cands[u]))
                go()
                if take:
                    for u in range(2):
                        link.need(m[u])
                        m[u] = link.did(dve.match_replace(cand2[:, u, :], val[:, u, 0:8], cands[u], -1.0))
                go()
                if take:
                    for u in range(2):
                        link.need(m[u])
                        m[u] = link.did(dve.max(val[:, u, 8:16], cand2[:, u, :]))
                go()
                if take:
                    link.wait()
                    m = link.did(dve.tensor_scalar(valid[:, :, :], val[:, :, :], 0.0, None, ALU.is_gt))
                    link.did(dve.tensor_scalar(V[:, :, 0:SLOTS], val[:, :, :], 1.0, -float(N // 2 + 1), ALU.max, ALU.add))
                if within(i, -4):
                    inverse_std(i - 4)
                if take:
                    link.need(m)
                    link.did(dve.tensor_reduce(pair(cnt, i), valid[:, :, :], AX, ALU.add))
                    link.wait()
                    dve.tensor_copy(V[:, :, 18], pair(cnt, i)).then_inc(counted, 1)
                if fill:
                    scan_max(i - 2, q, 1)

            def spans(i):
                dve.wait_ge(start_made, i + 1)
                wait(dve, cut_made, i * 2)
                link = Chain(dve, c_span)
                a = link.did(dve.tensor_scalar(carry[:, :], list_ps[:, 2:3], -float(SHARE * P), 0.0, ALU.add, ALU.max))
                link.did(dve.tensor_copy(start[:, bass.ds(i * 2, 1)], list_ps[:, 0:1]))
                link.need(a)
                a = link.did(dve.tensor_scalar(start[:, bass.ds(i * 2 + 1, 1)], list_ps[:, 1:2], carry[:, :], None, ALU.add))
                link.need(a)
                b = link.did(dve.tensor_copy(V[:, :, 16], pair(start, i)))
                c = link.did(dve.tensor_tensor(pair(end, i), pair(start, i), pair(cnt, i), ALU.add))
                for u in range(2):
                    link.did(dve.tensor_scalar(ge_s[:, u, 2:E2], iota_e[:, :], start[:, bass.ds(i * 2 + u, 1)], None, ALU.is_ge))
                link.need(b)
                link.did(dve.tensor_scalar(NV[:, :, 0:19], V[:, :, 0:19], -1.0, None, ALU.mult))
                link.need(c)
                for u in range(2):
                    ins = dve.tensor_scalar(ge_e[:, u, 2:E2], iota_e[:, :], end[:, bass.ds(i * 2 + u, 1)], None, ALU.is_ge)
                    if u == 0:
                        link.did(ins)
                link.wait()
                ins.then_inc(spans_made, 1)

            def lists(i, q):
                take, fill = within(i, 0), within(i, -1)
                if fill:
                    row_ends(i - 1, 1 - q, 0, 0)
                if take:
                    dve.wait_ge(lists_made, i + 1)
                    link = Chain(dve, c_list)
                    over_slots = lambda v: v.rearrange("p (b s) -> p b s", s=1).broadcast_to([P, 2 * BLOCKS, SLOTS])
                    link.did(dve.tensor_tensor(kpos[:, :].rearrange("p (u b) -> p u b", u=2),
                                               edge_pb.rearrange("p (u b) -> p u b", u=1).broadcast_to([P, 2, BLOCKS]),
                                               LB[:, :, 16].rearrange("p (u b) -> p u b", u=2), ALU.subtract))
                if fill:
                    row_ends(i - 1, 1 - q, 0, 1)
                if take:
                    link.wait()
                    link.did(dve.tensor_tensor(onehot[:, :, :], slot_iota.rearrange("p (b s) -> p b s", b=1).broadcast_to([P, 2 * BLOCKS, SLOTS]),
                                               over_slots(kpos[:, :]), ALU.is_equal))
                if fill:
                    row_ends(i - 1, 1 - q, 1, 0)
                if take:
                    link.wait()
                    link.did(dve.tensor_tensor(pick[:, :, :], onehot[:, :, :], LB[:, :, 0:SLOTS], ALU.mult))
                    link.did(dve.scalar_tensor_tensor(lastm[:, :], kpos[:, :], 1.0, LB[:, :, 18], ALU.add, ALU.is_equal))
                if within(i, 2) and not early(i):
                    clear_diagonal(i + 2, q, 1)
                if take:
                    link.wait()
                    link.did(dve.tensor_reduce(red[:, :], pick[:, :, :], AX, ALU.add))
                    dve.tensor_tensor(pair(last_row, i).rearrange("p a b -> p (a b)"), lastm[:, :], LB[:, :, 17], ALU.mult).then_inc(lists_taken, 1)
                if take:
                    link.wait()
                    link.did(dve.tensor_tensor(red[:, SHARE:SHARE + 1], red[:, SHARE:SHARE + 1], red[:, BLOCKS:BLOCKS + 1], ALU.add))
                if fill:
                    row_ends(i - 1, 1 - q, 1, 1)
                if take:
                    link.wait()
                    dve.tensor_scalar(idx[q][:, :], red[:, :], float(N // 2), float(N - 1), ALU.add, ALU.min).then_inc(idx_ready, 1)
                    dve.tensor_scalar(pair(idx_all, i).rearrange("p a b -> p (a b)"), red[:, :], float(N // 2), float(N - 1), ALU.add, ALU.min).then_inc(idx_kept, 1)

            clear_diagonal(0, 0, 0)
            relu_norm(2)
            relu_norm(3)
            clear_diagonal(0, 0, 1)
            dve.memset(ge_s[:, :, 0:2], 0.0)
            dve.memset(ones[:, :], 1.0)
            dve.memset(ones_h[:, :], 1.0)
            dve.memset(cut_w[:, 0, :], -HMAX)
            dve.memset(cut_w[:, 1, :], HMAX)
            dve.tensor_copy(tri[:, :], cst[:, C_TRI:C_TRI + P])
            dve.tensor_copy(iota_e[:, :], cst[:, C_IOTA:C_IOTA + EDGES])
            for u in range(2):
                dve.tensor_copy(V[:, u, 17:18], cst[:, C_P1:C_P1 + 1]).then_inc(cst_made, 1)
            dve.wait_ge(cst_made, 3)

            def step(i, q):
                read_keys(i, q)
                if early(i) and i > 0:
                    for u in range(2):
                        clear_diagonal(i + 1, 1 - q, u)
                if within(i, 0):
                    spans(i)
                if within(i, 2) and not early(i):
                    clear_diagonal(i + 2, q, 0)
                lists(i, q)
                if isinstance(i, int) and i == 0:
                    for u in range(2):
                        clear_diagonal(1, 1, u)
            steps(dve, step, PAIRS + 4, LEAD, 2)

            link = Chain(dve, c_set)
            dve.wait_ge(signed, 2 * T)
            link.then(dve.tensor_tensor(bad[:, 0, :], deg[:, :, 0], deg[:, :, 1], ALU.add))
            link.then(dve.scalar_tensor_tensor(bad[:, 0, :], cnt[:, :], -0.25, bad[:, 0, :], ALU.mult, ALU.add))
            link.then(dve.tensor_scalar(bad[:, 0, :], bad[:, 0, :], -(N * BASE + 0.25), None, ALU.add))
            link.then(dve.tensor_tensor(bad[:, 0, :], bad[:, 0, :], bad[:, 0, :], ALU.mult))
            link.did(dve.tensor_scalar(bad[:, 0, :], bad[:, 0, :], 0.01, None, ALU.is_ge))
            link.did(dve.tensor_scalar(bad[:, 1, :], cnt[:, :], float(SLOTS), None, ALU.is_ge))
            link.did(dve.tensor_scalar(bad[:, 2, :], rest[:, :], float(GROUPS), None, ALU.is_ge))
            link.then(dve.tensor_scalar(bad[:, 3, :], end[:, :], float(EDGES), None, ALU.is_gt))
            dve.tensor_reduce(bad_row[:, :], bad[:, :, :].rearrange("p c t -> p (c t)"), AX, ALU.add).then_inc(checked, 1)
            dve.wait_ge(bad_summed, 1)
            dve.tensor_copy(general[:, :], list_ps[:, 0:1]).then_inc(flag_made, 1)

            def copy_idx(i, q):
                wait(dve, tb_made, i * 2 - 2)
                dve.tensor_copy(idx[q][:, :], pair(idx_all, i).rearrange("p a b -> p (a b)")).then_inc(idx2_ready, 1)

            dve.wait_ge(idx_kept, PAIRS)
            copy_idx(0, 0)
            copy_idx(1, 1)
            dve.wait_ge(emb_saved, PAIRS)
            tgt, src = EN[:, :, D], EN[:, :, D + 1]
            link = Chain(dve, c_set)
            link.did(dve.tensor_scalar(src01[:, :], src, NEG_SLOPE, None, ALU.mult))
            link.then(dve.tensor_tensor(junk[:, 0:T], tgt, src, ALU.add))
            dve.scalar_tensor_tensor(xself[:, :], junk[:, 0:T], NEG_SLOPE, junk[:, 0:T], ALU.mult, ALU.max).then_inc(self_made, 1)

            def off_part(link, t, part):
                if isinstance(t, int) and t >= T:
                    return
                if part == 0:
                    link.did(dve.tensor_scalar(off_s[:, :], iota_e[:, :], start[:, bass.ds(t, 1)], -BIG, ALU.is_lt, ALU.mult))
                if part == 1:
                    link.did(dve.tensor_scalar(off_e[:, :], iota_e[:, :], end[:, bass.ds(t, 1)], -BIG, ALU.is_ge, ALU.mult))
                if part == 2:
                    link.did(dve.tensor_tensor(off[:, :], off_s[:, :], off_e[:, :], ALU.add))

            def tile1(t, u):
                has = not isinstance(t, int)
                now, p, f = has or t < T, has or 1 <= t <= T, has or 2 <= t
                tt = bass.ds(t, 1)
                if now:
                    dve.wait_ge(tb_made, t + 1)
                link = Chain(dve, c_z)
                if now:
                    k = link.did(dve.tensor_tensor_reduce(z[:, u, :], off[:, :], tb_ps[u][:, 0:EDGES], 1.0, -3e38, ALU.add, ALU.max, zmax[:, :]))
                if p:
                    dve.wait_ge(exps_made, t)
                    wait(dve, probT_made, t - 2)
                    dve.scalar_tensor_tensor(prob[:, 1 - u, :], exp_pos[:, 1 - u, :], 0.0, exp_neg[:, 1 - u, :], ALU.max, ALU.max,
                                             accum_out=den[:, 1 - u:2 - u]).then_inc(probs_made, 1)
                if now:
                    link.need(k)
                    dve.sem_inc(z_made)
                    k = link.did(dve.tensor_scalar(lin[:, 0:1], zmax[:, :], tile(EN, t, slice(D + 1, D + 2)), None, ALU.add))
                if f:
                    g = t - 2
                    dve.wait_ge(num_made, t - 1)
                    d = link.did(dve.tensor_tensor(dn[:, 0:1], den[:, u:u + 1], wself[:, u:u + 1], ALU.add))
                    dve.scalar_tensor_tensor(num[:, 0, :], tile(EN, g, slice(0, D)), wself[:, u:u + 1],
                                             seg_ps[:, 0:D], ALU.mult, ALU.add).then_inc(num_taken, 1)
                if now:
                    link.need(k)
                    k = link.did(dve.scalar_tensor_tensor(lin[:, 1:2], lin[:, 0:1], NEG_SLOPE, lin[:, 0:1], ALU.mult, ALU.max))
                if now:
                    off_part(link, t + 1, 0)
                if now:
                    link.need(k)
                    k = link.did(dve.tensor_scalar(neg_max[:, u:u + 1], lin[:, 1:2], xself[:, tt], -1.0, ALU.max, ALU.mult))
                if f:
                    link.need(d)
                    link.did(dve.reciprocal(dn[:, 1:2], dn[:, 0:1]))
                if now:
                    link.need(k)
                    dve.tensor_tensor(bias[:, u, 0:1], neg_max[:, u:u + 1], tile(EN, t, slice(D + 1, D + 2)), ALU.add)
                    dve.tensor_tensor(bias[:, u, 1:2], neg_max[:, u:u + 1], src01[:, tt], ALU.add).then_inc(m_made, 1)
                if f:
                    link.wait()
                    dve.wait_ge(num_taken, t - 1)
                    link.did(dve.tensor_scalar(num[:, 1, :], num[:, 0, :], dn[:, 1:2], 0.0, ALU.mult, ALU.max))
                if now:
                    off_part(link, t + 1, 1)
                if f:
                    link.wait()
                    if has or g >= 2:
                        dve.wait_ge(out_stored[u], (g - u) * 8)
                    dve.tensor_tensor(O[:, u, :], num[:, 1, :], tile(X, g), ALU.add).then_inc(out_made, 1)
                if now:
                    link.wait()
                    off_part(link, t + 1, 2)
                link.wait()

            link = Chain(dve, c_z)
            for part in range(3):
                link.wait()
                off_part(link, 0, part)
            link.wait()

            def step1(i, q):
                tile1(i * 2, 0)
                tile1(i * 2 + 1, 1)
                if within(i, 2) and not (isinstance(i, int) and i + 2 >= PAIRS):
                    copy_idx(i + 2, q)
            steps(dve, step1, PAIRS, 3, 2)
            tile1(T, 0)
            tile1(T + 1, 1)

            with dve.If(flag(dve) > 0):
                dve.sem_inc(grow_used)
                dve.sem_inc(gout_stored, 16)
                with dve.Fori(0, T) as t:
                    link = Chain(dve, c_gen)
                    link.then(dve.tensor_copy(h1, tile(H, t)))
                    dve.sem_inc(gh_ready)
                    dve.wait_ge(ghT_ps, t + 1)
                    link.then(dve.tensor_copy(hT[:, bass.ds(t * P, P)], emb_ps[:, 0:P]))
                dve.wait_ge(gx_in, 16)
                with dve.Fori(0, T) as t:
                    with dve.Fori(0, P // 2) as duo:
                        for u in range(2):
                            dve.wait_ge(grow_in[u], (t * (P // 2) + duo) * 16 + 16)
                            link = Chain(dve, c_gen)
                            link.then(dve.scalar_tensor_tensor(wide, row_in[:, u, :], 0.0, hT, ALU.not_equal, ALU.mult))
                            dve.sem_inc(grow_used)
                            link.then(dve.tensor_reduce(aggT[:, bass.ds(duo * 2 + u, 1)], wide, AX, ALU.max))
                    dve.sem_inc(gmax_made)
                    dve.wait_ge(gagg_made, t + 1)
                    link = Chain(dve, c_gen)
                    link.then(dve.tensor_tensor(tile(X, t), tile(X, t), seg_ps[:, 0:D], ALU.add))
                with dve.Fori(0, T) as t:
                    link = Chain(dve, c_gen)
                    link.then(dve.bn_stats(stat6[:, 0, :], tile(X, t)))
                    link.then(dve.bn_aggr(mv1[:, 0, :], stat6[:, 0, :]))
                    link.then(dve.tensor_scalar(nmr[:, bass.ds(t, 1)], mv1[:, 0, 0:1], -1.0, None, ALU.mult))
                    dve.sem_inc(gvar_made)
                    dve.wait_ge(gstd_made, t + 1)
                    link.then(dve.reciprocal(rstd[:, bass.ds(t, 1)], std[:, bass.ds(t, 1)]))
                    dve.wait_ge(gemb_ps, t + 1)
                    link.then(dve.tensor_scalar(tile(EN, t), emb_ps[:, P:P + D + 2], rstd[:, bass.ds(t, 1)], None, ALU.mult))
                    link.then(dve.tensor_copy(zmax[:, :], tile(EN, t, slice(D, D + 1))))
                    dve.sem_inc(gt_ready)
                    dve.wait_ge(gt_ps_made, t + 1)
                    link.then(dve.tensor_copy(t_all[:, bass.ds(t * P, P)], seg_ps[:, 0:P]))
                dve.sem_inc(gadj_used)
                with dve.Fori(0, T) as t:
                    dve.wait_ge(gadj_in, t * 16 + 16)
                    link = Chain(dve, c_gen)
                    link.then(dve.tensor_scalar(e_wide, t_all, tile(EN, t, slice(D + 1, D + 2)), None, ALU.add))
                    link.then(dve.scalar_tensor_tensor(e_wide, e_wide, NEG_SLOPE, e_wide, ALU.mult, ALU.max))
                    link.then(dve.scalar_tensor_tensor(e_wide, row_in[:, 0, :], 0.0, e_wide, ALU.is_gt, ALU.mult))
                    link.then(dve.tensor_scalar(wide, row_in[:, 0, :], 0.0, 1.0, ALU.is_gt, ALU.subtract))
                    link.then(dve.scalar_tensor_tensor(e_wide, wide, -MASKED, e_wide, ALU.mult, ALU.add))
                    dve.sem_inc(gadj_used)
                    link.then(dve.tensor_reduce(zmax[:, :], e_wide, AX, ALU.max))
                    link.then(dve.tensor_scalar(neg_max[:, 0:1], zmax[:, :], -1.0, None, ALU.mult))
                    dve.sem_inc(gmax1_made)
                    dve.wait_ge(gprob_made, t + 1)
                    settled(dve, "dve")
                    with dve.Fori(0, T) as j:
                        link = Chain(dve, c_gen)
                        link.then(dve.tensor_copy(h1, e_wide[:, bass.ds(j * P, P)]))
                        dve.sem_inc(gprob_ready)
                        dve.wait_ge(gprobT_ps, t * T + j + 1)
                        link.then(dve.tensor_copy(h1T, emb_ps[:, 0:P]))
                        dve.sem_inc(gprobT_saved)
                    dve.wait_ge(gnum_made, t + 1)
                    link = Chain(dve, c_gen)
                    link.then(dve.reciprocal(dn[:, 1:2], den[:, 0:1]))
                    link.then(dve.tensor_scalar(num[:, 1, :], seg_ps[:, 0:D], dn[:, 1:2], 0.0, ALU.mult, ALU.max))
                    dve.wait_ge(gout_stored, t * 16 + 16)
                    link.then(dve.tensor_tensor(O[:, 0, :], num[:, 1, :], tile(X, t), ALU.add))
                    dve.sem_inc(gout_made)

        @block.tensor
        def _(pe):
            pe.wait_ge(cst_made, 1)
            pe.wait_ge(w_in, 48)
            pe.transpose(emb_ps[:, 0:D], Wsb[:, :], ident)
            pe.matmul(emb_ps[:, D:D + 1], Wsb[:, :], asb[:, 1:2], start=True, stop=True)
            pe.matmul(emb_ps[:, D + 1:D + 2], Wsb[:, :], asb[:, 0:1], start=True, stop=True).then_inc(wx_ps_made, 1)

            def codes(i, q, u):
                pe.wait_ge(diag_cleared, i * 2 + u + 1)
                if u == 0:
                    wait(pe, keys_taken, i)
                keys = key_ps[:, u * GROUPS:(u + 1) * GROUPS]
                pe.matmul(keys, ones_b[:, :], key_row[:, :], start=True, stop=False)
                for k in range(BITS):
                    ins = pe.matmul(keys, code_w[:, k, :], mask[:, q, u, k * GROUPS:(k + 1) * GROUPS], start=False, stop=(k == BITS - 1))
                ins.then_inc(keys_made, 1)
            codes(0, 0, 0)
            codes(0, 0, 1)

            def turn_gathered(i, q, u):
                wait(pe, scanned, i * 2 + u)
                for b in range(BLOCKS):
                    pe.wait_ge(gathered[q][u * SHARE + b], (i - q) * 8 + 16)
                    ins = pe.transpose(gt_ps[:, b * P:(b + 1) * P], G[:, q, u * SHARE + b, 0:D], ident)
                ins.then_inc(gt_made, 1)

            def turn_back(i, u):
                pe.wait_ge(scanned, i * 2 + u + 1)
                for b in range(BLOCKS):
                    ins = pe.transpose(back_ps[:, b * P:(b + 1) * P], scan[:, b * P:(b + 1) * P], ident)
                ins.then_inc(back_made, 1)

            def pick_ends(i, q, u):
                pe.wait_ge(back_saved, i * 2 + u + 1)
                pe.wait_ge(ends_made, i * 4 + u * 2 + 2)
                if u == 0:
                    wait(pe, seg_taken, i)
                for b in range(BLOCKS):
                    ins = pe.matmul(seg_ps[:, u * D:(u + 1) * D], S[:, q, u, b, :], scanT[:, u, b, :], start=(b == 0), stop=(b == BLOCKS - 1))
                ins.then_inc(seg_made, 1)

            def cuts(i, u):
                for lo, hi in ((0, 512), (512, EDGES)):
                    pe.matmul(back_ps[:, lo:hi], cut_w[:, 0, :], ge_s[:, u, lo + 2:hi + 2], start=True, stop=False)
                    ins = pe.matmul(back_ps[:, lo:hi], cut_w[:, 1, :], ge_s[:, u, lo + 1:hi + 1], start=False, stop=True)
                ins.then_inc(cut_made, 1)

            def step(i, q):
                p, e = i - 2, i - 4
                if within(i, -2):
                    turn_gathered(p, q, 0)
                if within(i, 1) and not early(i):
                    codes(i + 1, 1 - q, 0)
                if within(i, -2):
                    if not isinstance(i, int):
                        pe.wait_ge(cut_saved, i * 2)
                    else:
                        wait(pe, cut_saved, min(i, PAIRS) * 2)
                    turn_back(p, 0)
                if within(i, -4):
                    pe.wait_ge(h1_made, e + 1)
                    if isinstance(e, int) and e == 0:
                        pe.wait_ge(wx_saved, 1)
                    wait(pe, emb_saved, e)
                    for u in range(2):
                        ins = pe.transpose(emb_ps[:, u * P:(u + 1) * P], h1p[:, u, :], ident)
                    ins.then_inc(h1T_made, 1)
                if within(i, -2):
                    turn_gathered(p, q, 1)
                if within(i, 1) and not early(i):
                    codes(i + 1, 1 - q, 1)
                if within(i, -4):
                    pe.wait_ge(h1T_saved, e + 1)
                    for u in range(2):
                        ins = pe.matmul(emb_ps[:, u * (D + 2):(u + 1) * (D + 2)], h1Tp[:, u, :], WX[:, :], start=True, stop=True)
                    ins.then_inc(emb_made, 1)
                if within(i, 0):
                    pe.wait_ge(counted, i + 1)
                    wait(pe, lists_taken, i)
                    pe.matmul(list_ps[:, 0:2], tri[:, :], V[:, :, 18], start=True, stop=True)
                    pe.matmul(list_ps[:, 2:3], ones_h[:, :], V[:, 0, 18:19], start=True, stop=True).then_inc(start_made, 1)
                if within(i, -2):
                    pick_ends(p, q, 0)
                    turn_back(p, 1)
                if within(i, 0):
                    pe.wait_ge(spans_made, i + 1)
                    for u in range(2):
                        for b in range(BLOCKS):
                            at = 8 + 20 * (u * BLOCKS + b)
                            edges = slice(2 + b * P, 2 + (b + 1) * P)
                            pe.matmul(list_ps[:, at:at + 19], ge_s[:, u, edges], V[:, u, 0:19], start=True, stop=False)
                            ins = pe.matmul(list_ps[:, at:at + 19], ge_e[:, u, edges], NV[:, u, 0:19], start=False, stop=True)
                    ins.then_inc(lists_made, 1)
                if within(i, -2):
                    pick_ends(p, q, 1)
                if early(i):
                    codes(i + 1, 1 - q, 0)
                    codes(i + 1, 1 - q, 1)
                if within(i, 0):
                    if not within(i, -2):
                        wait(pe, cut_saved, i * 2)
                    cuts(i, 0)
                    pe.wait_ge(cut_saved, i * 2 + 1)
                    cuts(i, 1)
            steps(pe, step, PAIRS + 4, LEAD, 2)

            pe.wait_ge(checked, 1)
            pe.matmul(list_ps[:, 0:1], ones[:, :], bad_row[:, :], start=True, stop=True).then_inc(bad_summed, 1)

            def targets(t, q, u):
                wait(pe, z_made, t - 1)
                for b in range(BLOCKS):
                    pe.wait_ge(gathered[q][u * SHARE + b], (t - u - 2 * q) * 4 + 16 * (PAIRS // 2) + 16)
                    ins = pe.matmul(tb_ps[u][:, b * P:(b + 1) * P], G[:, q, u * SHARE + b, D:D + 1].broadcast_to([P, P]), ident, start=True, stop=True)
                ins.then_inc(tb_made, 1)

            def turn_prob(t, u):
                pe.wait_ge(probs_made, t + 1)
                wait(pe, probT_saved, t)
                for b in range(BLOCKS):
                    ins = pe.transpose(gt_ps[:, b * P:(b + 1) * P], prob[:, u, b * P:(b + 1) * P], ident)
                ins.then_inc(probT_made, 1)

            def product(t, q, u):
                pe.wait_ge(probT_saved, t + 1)
                wait(pe, num_taken, t)
                for b in range(BLOCKS):
                    ins = pe.matmul(seg_ps[:, 0:D], probT[:, u, b, :], G[:, q, u * SHARE + b, 0:D], start=(b == 0), stop=(b == BLOCKS - 1))
                ins.then_inc(num_made, 1)

            targets(0, 0, 0)

            def step1(i, q):
                if within(i, -1):
                    turn_prob(i * 2 - 1, 1)
                targets(i * 2 + 1, q, 1)
                if within(i, -1):
                    product(i * 2 - 1, 1 - q, 1)
                turn_prob(i * 2, 0)
                if within(i, 1):
                    targets(i * 2 + 2, 1 - q, 0)
                product(i * 2, q, 0)
            steps(pe, step1, PAIRS, 2, 2)
            turn_prob(T - 1, 1)
            product(T - 1, 1, 1)

            with pe.If(flag(pe) > 0):
                with pe.Fori(0, T) as t:
                    pe.wait_ge(gh_ready, t + 1)
                    pe.transpose(emb_ps[:, 0:P], h1, ident).then_inc(ghT_ps, 1)
                with pe.Fori(0, T) as t:
                    pe.wait_ge(gmax_made, t + 1)
                    pe.transpose(seg_ps[:, 0:D], aggT, ident).then_inc(gagg_made, 1)
                with pe.Fori(0, T) as t:
                    pe.wait_ge(gh1_made, t + 1)
                    pe.transpose(emb_ps[:, 0:P], h1, ident).then_inc(gh1T_ps, 1)
                    pe.wait_ge(gh1T_saved, t + 1)
                    pe.matmul(emb_ps[:, P:P + D + 2], h1T, WX[:, :], start=True, stop=True).then_inc(gemb_ps, 1)
                    pe.wait_ge(gt_ready, t + 1)
                    pe.matmul(seg_ps[:, 0:P], zmax[:, 0:1].broadcast_to([P, P]), ident, start=True, stop=True).then_inc(gt_ps_made, 1)
                with pe.Fori(0, T) as t:
                    def product(j, first, last):
                        pe.wait_ge(gprob_ready, t * T + j + 1)
                        pe.transpose(emb_ps[:, 0:P], h1, ident).then_inc(gprobT_ps, 1)
                        pe.wait_ge(gprobT_saved, t * T + j + 1)
                        ins = pe.matmul(seg_ps[:, 0:D], h1T, tile(EN, j, slice(0, D)), start=first, stop=last)
                        if last:
                            ins.then_inc(gnum_made, 1)
                    product(0, True, False)
                    with pe.Fori(0, T - 2) as j:
                        product(j + 1, False, False)
                    product(T - 1, False, True)


def kernel(**inputs):
    import numpy as _np
    import concourse.bacc as _bacc
    from concourse import mybir as _mybir
    from concourse.bass_utils import run_bass_kernel_spmd as _run

    nc = _bacc.Bacc("TRN2", target_bir_lowering=False, num_devices=1)
    arrays, args = {}, []
    given = {n: inputs[n] for n in ("x", "adj", "L1_gnn_W", "L1_gnn_a")}
    given["constants"] = constants()
    for name, value in given.items():
        a = _np.ascontiguousarray(value)
        arrays[f"in_{name}_dram"] = a
        args.append(nc.dram_tensor(f"in_{name}_dram", a.shape, _mybir.dt.from_np(a.dtype), kind="ExternalInput").ap())
    args.append(nc.dram_tensor("out_0_dram", (N, D), _mybir.dt.float32, kind="ExternalOutput").ap())
    args.append(nc.dram_tensor("h_rows", (N, D), _mybir.dt.float32, kind="Internal").ap())
    args.append(nc.dram_tensor("e_rows", (N, ROWLEN), _mybir.dt.float32, kind="Internal").ap())
    build(nc, *args)
    r = _run(nc, [arrays], core_ids=[0])
    return r.results[0]["out_0_dram"]
```
